# Optimizing a Trainium2 kernel written in Bass

```python
import numpy as np
import jax
import jax.numpy as jnp

def _softmax(x, axis=-1):
    return jax.nn.softmax(x, axis=axis)

def _gelu(x):
    return jax.nn.gelu(x, approximate=True)

def _silu(x):
    return jax.nn.silu(x)

def _sigmoid(x):
    return jax.nn.sigmoid(x)

def _layernorm(x, axis=-1, eps=1e-05):
    m = jnp.mean(x, axis=axis, keepdims=True)
    v = jnp.var(x, axis=axis, keepdims=True)
    return (x - m) / jnp.sqrt(v + eps)

def _scatter_add(tgt, idx, src, axis=0):
    return tgt.at[idx].add(src)

def _segment_sum(src, seg, n):
    return jax.ops.segment_sum(src, seg, n)
kernel_name = 'mk_flamingo_gated_d1_seqx_r8_17880a'

def setup_inputs(seed: int=0):
    np.random.seed(seed)
    _w = jnp.asarray

    def _rec_inputs():
        import jax
        import jax.numpy as jnp
        _rk = jax.random.key(seed)
        x = -0.0002928 + 1 * jax.random.normal(jax.random.fold_in(_rk, 1), (32, 128, 128), jnp.float32)
        _lenS = 128 - jax.random.randint(jax.random.fold_in(_rk, 7), (32,), 0, max(1, 128 // 4) + 1, jnp.int32)
        _lenS2 = 128 - jax.random.randint(jax.random.fold_in(_rk, 8), (32,), 0, max(1, 128 // 4) + 1, jnp.int32)
        _ctx_1024P = jax.random.normal(jax.random.fold_in(_rk, 11), (32, 16, 128), jnp.float32)
        _ctx_1024c = jax.random.dirichlet(jax.random.fold_in(_rk, 511), 0.3 * jnp.ones((16,), jnp.float32), (32, 128))
        _ctx_1024t = jnp.einsum('bsk,bkd->bsd', _ctx_1024c, _ctx_1024P)
        _ctx_1024t = _ctx_1024t * jax.lax.rsqrt(jnp.mean(jnp.square(_ctx_1024t)) + 1e-12) * 0.953939
        ctx_1024 = -1.39393e-06 + 0.999914 * (_ctx_1024t + 0.3 * jax.random.normal(jax.random.fold_in(_rk, 611), (32, 128, 128), jnp.float32))
        _validS = jnp.arange(128)[None, :] < _lenS[:, None]
        _validS2 = jnp.arange(128)[None, :] < _lenS2[:, None]
        _causal = jnp.tril(jnp.ones((128, 128), dtype=bool))
        mask_BxS2_bf0 = jnp.logical_not(jnp.ones((32, 128), dtype=bool))
        _g = jax.random.normal(jax.random.fold_in(_rk, 9001), (2, 1), jnp.float32)
        _g = jnp.sign(_g) * jnp.maximum(jnp.abs(_g), 1.0) + (_g == 0) * 1.0
        g_xattn = _g[0]
        g_ffn = _g[1]
        return (x, ctx_1024, mask_BxS2_bf0, g_xattn, g_ffn)
    x, ctx_1024, mask_BxS2_bf0, g_xattn, g_ffn = _rec_inputs()

    def _L0_xattn_setup():
        import jax, jax.numpy as jnp
        import numpy as np
        DIM = 128
        HEADS = 16
        DIM_HEAD = 64
        INNER = HEADS * DIM_HEAD
        B, N = (2, 256)
        SCALE = DIM_HEAD ** (-0.5)
        key = jax.random.key(seed)
        ks = jax.random.split(key, 9)
        s_in = 1.0 / np.sqrt(DIM)
        s_inner = 1.0 / np.sqrt(INNER)
        return {'q': jax.random.normal(ks[0], (B, N, DIM), jnp.float32), 'k': jax.random.normal(ks[1], (B, N, DIM), jnp.float32), 'v': jax.random.normal(ks[2], (B, N, DIM), jnp.float32), 'Wq': jax.random.normal(ks[3], (DIM, INNER), jnp.float32) * s_in, 'Wk': jax.random.normal(ks[4], (DIM, INNER), jnp.float32) * s_in, 'Wv': jax.random.normal(ks[5], (DIM, INNER), jnp.float32) * s_in, 'Wo': jax.random.normal(ks[6], (INNER, DIM), jnp.float32) * s_inner, 'bo': jax.random.normal(ks[7], (DIM,), jnp.float32) * s_inner, 'mask': jnp.zeros((B, N), dtype=bool)}
    _L0_xattn_all = _L0_xattn_setup()
    _L0_xattn_in = {k: v for k, v in _L0_xattn_all.items() if k in ('Wq', 'Wk', 'Wv', 'Wo', 'bo')}
    del _L0_xattn_all

    def _L0_ffn_setup():
        import jax, jax.numpy as jnp
        import numpy as np
        BITS = 8
        LORA_RANK = 16
        LORA_ALPHA = 32
        SCALING = LORA_ALPHA / LORA_RANK

        def fake_quant_weight(w, bits=BITS):
            qmax = 2.0 ** (bits - 1) - 1
            scale = jnp.max(jnp.abs(w)) / qmax
            wq = jnp.clip(jnp.round(w / scale), -qmax - 1, qmax) * scale
            return w + jax.lax.stop_gradient(wq - w)

        def qat_lora_linear(x, W, b, A, B):
            Wq = fake_quant_weight(W)
            base = jnp.einsum('bsi,oi->bso', x, Wq) + b
            lora = jnp.einsum('bsr,or->bso', jnp.einsum('bsi,ri->bsr', x, A), B)
            return base + SCALING * lora
        key = jax.random.key(seed)
        ks = jax.random.split(key, 9)
        d, f = (128, 512)
        s_in = 1.0 / np.sqrt(d)
        s_ff = 1.0 / np.sqrt(f)
        return {'hidden_states': jax.random.normal(ks[0], (4, 256, d), jnp.float32), 'W_fc': jax.random.normal(ks[1], (f, d), jnp.float32) * s_in, 'b_fc': jnp.zeros((f,), jnp.float32), 'A_fc': jax.random.normal(ks[2], (LORA_RANK, d), jnp.float32) * s_in, 'B_fc': jnp.zeros((f, LORA_RANK), jnp.float32), 'W_proj': jax.random.normal(ks[3], (d, f), jnp.float32) * s_ff, 'b_proj': jnp.zeros((d,), jnp.float32), 'A_proj': jax.random.normal(ks[4], (LORA_RANK, f), jnp.float32) * s_ff, 'B_proj': jnp.zeros((d, LORA_RANK), jnp.float32)}
    _L0_ffn_all = _L0_ffn_setup()
    _L0_ffn_in = {k: v for k, v in _L0_ffn_all.items() if k in ('W_fc', 'b_fc', 'A_fc', 'B_fc', 'W_proj', 'b_proj', 'A_proj', 'B_proj')}
    del _L0_ffn_all
    return {'x': x, 'ctx_1024': ctx_1024, 'mask_BxS2_bf0': mask_BxS2_bf0, 'g_xattn': g_xattn, 'g_ffn': g_ffn, 'L0_xattn_Wq': _L0_xattn_in['Wq'], 'L0_xattn_Wk': _L0_xattn_in['Wk'], 'L0_xattn_Wv': _L0_xattn_in['Wv'], 'L0_xattn_Wo': _L0_xattn_in['Wo'], 'L0_xattn_bo': _L0_xattn_in['bo'], 'L0_ffn_W_fc': _L0_ffn_in['W_fc'], 'L0_ffn_b_fc': _L0_ffn_in['b_fc'], 'L0_ffn_A_fc': _L0_ffn_in['A_fc'], 'L0_ffn_B_fc': _L0_ffn_in['B_fc'], 'L0_ffn_W_proj': _L0_ffn_in['W_proj'], 'L0_ffn_b_proj': _L0_ffn_in['b_proj'], 'L0_ffn_A_proj': _L0_ffn_in['A_proj'], 'L0_ffn_B_proj': _L0_ffn_in['B_proj']}

def reference(x, ctx_1024, mask_BxS2_bf0, g_xattn, g_ffn, L0_xattn_Wq, L0_xattn_Wk, L0_xattn_Wv, L0_xattn_Wo, L0_xattn_bo, L0_ffn_W_fc, L0_ffn_b_fc, L0_ffn_A_fc, L0_ffn_B_fc, L0_ffn_W_proj, L0_ffn_b_proj, L0_ffn_A_proj, L0_ffn_B_proj):
    import jax
    import jax.numpy as jnp

    def _L0_xattn_ref(q, k, v, Wq, Wk, Wv, Wo, bo, mask):
        import jax, jax.numpy as jnp
        import numpy as np
        DIM = 128
        HEADS = 16
        DIM_HEAD = 64
        INNER = HEADS * DIM_HEAD
        B, N = (2, 256)
        SCALE = DIM_HEAD ** (-0.5)
        b, n, _ = q.shape
        h, d = (HEADS, DIM_HEAD)

        def split_heads(x):
            return x.reshape(b, n, h, d).transpose(0, 2, 1, 3)
        qh = split_heads(q @ Wq)
        kh = split_heads(k @ Wk)
        vh = split_heads(v @ Wv)
        dots = jnp.einsum('bhid,bhjd->bhij', qh, kh) * SCALE
        mask_value = -jnp.finfo(dots.dtype).max
        dots = jnp.where(mask[:, None, None, :], mask_value, dots)
        causal = jnp.triu(jnp.ones((n, n), dtype=bool), k=1)
        dots = jnp.where(causal[None, None, :, :], mask_value, dots)
        attn = jax.nn.softmax(dots, axis=-1)
        out = jnp.einsum('bhij,bhjd->bhid', attn, vh)
        out = out.transpose(0, 2, 1, 3).reshape(b, n, h * d)
        return out @ Wo + bo

    def _L0_ffn_ref(hidden_states, W_fc, b_fc, A_fc, B_fc, W_proj, b_proj, A_proj, B_proj):
        import jax, jax.numpy as jnp
        import numpy as np
        BITS = 8
        LORA_RANK = 16
        LORA_ALPHA = 32
        SCALING = LORA_ALPHA / LORA_RANK

        def fake_quant_weight(w, bits=BITS):
            qmax = 2.0 ** (bits - 1) - 1
            scale = jnp.max(jnp.abs(w)) / qmax
            wq = jnp.clip(jnp.round(w / scale), -qmax - 1, qmax) * scale
            return w + jax.lax.stop_gradient(wq - w)

        def qat_lora_linear(x, W, b, A, B):
            Wq = fake_quant_weight(W)
            base = jnp.einsum('bsi,oi->bso', x, Wq) + b
            lora = jnp.einsum('bsr,or->bso', jnp.einsum('bsi,ri->bsr', x, A), B)
            return base + SCALING * lora
        h = qat_lora_linear(hidden_states, W_fc, b_fc, A_fc, B_fc)
        h = jax.nn.gelu(h, approximate=False)
        h = qat_lora_linear(h, W_proj, b_proj, A_proj, B_proj)
        return h
    x = x + jnp.tanh(g_xattn[0]) * _L0_xattn_ref(_layernorm(x, axis=-1), ctx_1024, ctx_1024, L0_xattn_Wq, L0_xattn_Wk, L0_xattn_Wv, L0_xattn_Wo, L0_xattn_bo, mask_BxS2_bf0)
    x = x + jnp.tanh(g_ffn[0]) * _L0_ffn_ref(_layernorm(x, axis=-1), L0_ffn_W_fc, L0_ffn_b_fc, L0_ffn_A_fc, L0_ffn_B_fc, L0_ffn_W_proj, L0_ffn_b_proj, L0_ffn_A_proj, L0_ffn_B_proj)
    return x

_drawn_inputs = setup_inputs


def setup_inputs(seed=0):
    import zlib

    import numpy as np

    out = dict(_drawn_inputs(seed))
    spreads = {'L0_ffn_b_fc': (0.0, 0.1),
     'L0_ffn_B_fc': (0.0, 0.1),
     'L0_ffn_b_proj': (0.0, 0.1),
     'L0_ffn_B_proj': (0.0, 0.1)}
    factors = {}
    for name, (base, spread) in spreads.items():
        noise = np.random.default_rng([zlib.crc32(name.encode()), seed]).standard_normal(out[name].shape)
        drawn = base * np.exp(spread * noise) if base else spread * noise
        out[name] = jnp.asarray(drawn.astype(out[name].dtype))
    for name, factor in factors.items():
        out[name] = (out[name] * factor).astype(out[name].dtype)
    return out
```

```python
from contextlib import ExitStack

import concourse.bass as bass
import concourse.mybir as mybir
import numpy as np

F32 = mybir.dt.float32
F32R = mybir.dt.float32r
ALU = mybir.AluOpType
ACT = mybir.ActivationFunctionType
AX = mybir.AxisListType
RMAX = bass.bass_isa.ReduceOp.max

P = 128
BATCHES, HEADS, DH = 32, 16, 64
INNER = HEADS * DH
FF, RANK = 512, 16
CHUNKS = FF // P
SCALE = DH ** -0.5
EPS = 1e-5
FMAX = float(np.finfo(np.float32).max)
QMAX = 127.0
LORA_SCALE = 2.0
ROUND = 12582912.0

PAIRS = BATCHES // 2
STEP_HEADS = 8
STEPS = BATCHES * HEADS // STEP_HEADS
BODY = 8
LEAD = 3
JOBS = 14
JOB = [("turn", 0), ("turn", 1), ("u", 0), ("v", 0), ("u", 1), ("u", 2), ("v", 1),
       ("u", 3), ("u", 4), ("v", 2), ("u", 5), ("u", 6), ("u", 7), ("v", 3)]
SLOT_JOBS = [[0, 1, 2, 3], [4, 5, 6], [7, 8, 9], [10, 11, 12, 13]]
SPLITS = [n for n, (kind, _) in enumerate(JOB) if kind != "v"]
NSPLIT = len(SPLITS)
GROUPS = BATCHES // 4


def splits_before(n):
    return sum(m < n for m in SPLITS)


def exists(i, c, end=STEPS, per=BODY):
    return not isinstance(i, int) or 0 <= per * i + c < end


def build(nc, x, ctx, mask, g_xattn, g_ffn, Wq, Wk, Wv, Wo, bo, W_fc, b_fc, A_fc, B_fc, W_proj,
          b_proj, A_proj, B_proj, out):
    st = ExitStack()
    with st:
        def sb(name, shape, dt=F32):
            return st.enter_context(nc.sbuf_tensor(name, shape, dt))

        def sem(name):
            return st.enter_context(nc.semaphore(name))

        X = sb("X", [P, BATCHES * P])
        C = sb("C", [P, 2, 2 * P])
        maskb = sb("maskb", [P, BATCHES * P], mybir.dt.uint8)
        ident = sb("ident", [P, P])
        causal = sb("causal", [P, P])
        bias = sb("bias", [P, 2, P])
        xn = sb("xn", [P, 2, 2 * P])
        tT_hi = sb("tT_hi", [P, 2, 4 * P], F32R)
        tT_lo = sb("tT_lo", [P, 2, 4 * P], F32R)
        u_hi = sb("u_hi", [P, 2, HEADS, 2 * P], F32R)
        u_lo = sb("u_lo", [P, 2, HEADS, 2 * P], F32R)
        v = sb("v", [P, 2, 2, INNER])
        masked = sb("masked", [P, 2, STEP_HEADS, P])
        prob = sb("prob", [P, 2, STEP_HEADS, P])
        probT = sb("probT", [P, 2, STEP_HEADS, P])
        headT = sb("headT", [P, 2, 4 * P])
        rowmax = sb("rowmax", [P, 2, STEP_HEADS])
        negmax = sb("negmax", [P, 2, STEP_HEADS])
        rowsum = sb("rowsum", [P, 2, STEP_HEADS])
        invsum = sb("invsum", [P, 2, STEP_HEADS])
        stats = sb("stats", [P, 4, 6])
        meanvar = sb("meanvar", [P, 4, 2])
        rstd = sb("rstd", [P, 4])
        power = sb("power", [P, 4])
        M_hi = sb("M_hi", [P, HEADS, P], F32R)
        M_lo = sb("M_lo", [P, HEADS, P], F32R)
        Wv_raw = sb("Wv_raw", [P, INNER])
        Wv_hi = sb("Wv_hi", [P, INNER], F32R)
        Wv_lo = sb("Wv_lo", [P, INNER], F32R)
        Wo_sb = sb("Wo_sb", [P, INNER // P, P])
        gates = sb("gates", [P, 2])
        gbias = sb("gbias", [P, 2, P])
        Wf = sb("Wf", [P, 2, FF])
        Wt = sb("Wt", [P, 2, FF])
        W1_hi = sb("W1_hi", [P, FF], F32R)
        W1_lo = sb("W1_lo", [P, FF], F32R)
        W2T = sb("W2T", [P, CHUNKS, P])
        bfc = sb("bfc", [P, CHUNKS])
        Afc = sb("Afc", [RANK, P])
        Apr = sb("Apr", [RANK, FF])
        Bfc = sb("Bfc", [P, CHUNKS, RANK])
        Bpr = sb("Bpr", [P, RANK])
        BT = sb("BT", [RANK, FF + P])
        wabs = sb("wabs", [P, 6])
        wall = sb("wall", [P, 2])
        wscale = sb("wscale", [P, 4])
        Wq_sb, Wk_sb = (probT[:, n].rearrange("p h j -> p (h j)") for n in range(2))
        WqT, WkT = (prob[:, n] for n in range(2))
        hid = v[:, :].rearrange("p a b (f t) -> p a (b f) t", f=2)
        xn2 = masked[:, :].rearrange("p a (b c) j -> p a b (c j)", b=2)[:, :, 0]
        yout = masked[:, :].rearrange("p a (b c) j -> p a b (c j)", b=2)[:, :, 1]
        x2T_hi = u_hi[:, 0, 0:4].rearrange("p (a b) t -> p a (b t)", a=2)
        x2T_lo = u_lo[:, 0, 0:4].rearrange("p (a b) t -> p a (b t)", a=2)

        S0, S1, T0, T1, J0, J1, OB, YB = (
            st.enter_context(nc.psum_tensor(n, [P, 512], F32))
            for n in ("S0", "S1", "T0", "T1", "J0", "J1", "OB", "YB"))
        score_bank, turn_bank, job_bank = (S0, S1), (T0, T1), (J0, J1)

        (ld_wq, ld_wk, ld_x0, ld_c0, ld_x1, ld_c1, ld_mask, ld_wv, ld_wo, ld_bias, ld_gate, ld_ffn,
         ld_lora) = (sem(n) for n in (
             "ld_wq", "ld_wk", "ld_x0", "ld_c0", "ld_x1", "ld_c1", "ld_mask", "ld_wv", "ld_wo",
             "ld_bias", "ld_gate", "ld_ffn", "ld_lora"))
        (ident_set, consts_set, w_turned, wqT_ready, wkT_ready, m_ready, m_hi_ready, m_lo_ready,
         wv_hi_ready, wv_lo_ready, gates_ready, wo_ready, gbias_ready, bT_turned, bT_ready,
         lora_ready, wprep, wmax_ready, wm_turned, w1_hi_ready, w12_ready) = (sem(n) for n in (
             "ident_set", "consts_set", "w_turned", "wqT_ready", "wkT_ready", "m_ready",
             "m_hi_ready", "m_lo_ready", "wv_hi_ready", "wv_lo_ready", "gates_ready", "wo_ready",
             "gbias_ready", "bT_turned", "bT_ready", "lora_ready", "wprep", "wmax_ready",
             "wm_turned", "w1_hi_ready", "w12_ready"))
        (scores_done, masked_done, negmax_done, exp_done, inv_done, prob_done, turned_done,
         probT0_done, probT1_done, heads_done, headT_done, y_done, x_done, bias_done, job_done,
         job_hi_done, job_lo_done, ln_stats, ln_rstd, ln_done, resid_done) = (sem(n) for n in (
             "scores_done", "masked_done", "negmax_done", "exp_done", "inv_done", "prob_done",
             "turned_done", "probT0_done", "probT1_done", "heads_done", "headT_done", "y_done",
             "x_done", "bias_done", "job_done", "job_hi_done", "job_lo_done", "ln_stats", "ln_rstd",
             "ln_done", "resid_done"))
        (f_stats, f_rstd, f_norm, f_turned, f_hi, f_lo, f_up, f_gelu, f_down, f_out, f_resid,
         stored0, stored1) = (sem(n) for n in (
             "f_stats", "f_rstd", "f_norm", "f_turned", "f_hi", "f_lo", "f_up", "f_gelu", "f_down",
             "f_out", "f_resid", "stored0", "stored1"))
        stored = (stored0, stored1)
        passed = sem("passed")

        block = st.enter_context(nc.Block())

        x_v = x.rearrange("b p d -> p b d")
        c_v = ctx.rearrange("b p d -> p b d")
        out_v = out.rearrange("b p d -> p b d")
        X_b = X[:, :].rearrange("p (b d) -> p b d", d=P)
        FIRST = 4

        @block.sync
        def _(sp):
            sp.dma_start(Wk_sb, Wk).then_inc(ld_wk, 16)

            def load_ctx(i, c):
                if c >= 2:
                    sp.wait_ge(job_done, JOBS * (2 * i + c - 2) + 2)
                sp.dma_start(C[:, c % 2, :].rearrange("p (b d) -> p b d", d=P),
                             c_v[:, bass.ds(4 * i + 2 * c, 2), :]).then_inc((ld_c0, ld_c1)[c % 2], 16)

            load_ctx(0, 0)
            sp.dma_start(maskb[:, :], mask.rearrange("(a b) j -> a (b j)", a=1)
                         .to_broadcast([P, BATCHES * P])).then_inc(ld_mask, 16)
            sp.dma_start(Wo_sb[:, :, :], Wo.rearrange("(q p) d -> p q d", p=P)).then_inc(ld_wo, 16)
            sp.dma_start(Wf[:, 0, :].rearrange("p (c d) -> p c d", d=P),
                         W_fc.rearrange("(c p) d -> p c d", p=P)).then_inc(ld_ffn, 16)
            sp.dma_start(Wf[:, 1, :], W_proj).then_inc(ld_ffn, 16)
            load_ctx(0, 1)
            sp.dma_start(X_b[:, FIRST:BATCHES], x_v[:, FIRST:BATCHES]).then_inc(ld_x1, 16)

            with sp.Fori(0, PAIRS // 2 - 1) as i:
                load_ctx(i, 2)
                load_ctx(i, 3)

            def store(i, c):
                sp.wait_ge(f_out, 2 * i + c + 1)
                sp.dma_start(out_v[:, bass.ds(8 * i + 4 * c, 4), :],
                             yout[:, c % 2].rearrange("p (b d) -> p b d", d=P))\
                    .then_inc(stored[c % 2], 16)

            with sp.Fori(0, GROUPS // 2) as i:
                store(i, 0)
                store(i, 1)
            sp.wait_ge(stored0, 16 * GROUPS // 2)
            sp.wait_ge(stored1, 16 * GROUPS // 2)

        @block.gpsimd
        def _(pool):
            pool.memset(ident[:, :], 0.0).then_inc(ident_set, 1)
            pool.memset(causal[:, :], 0.0).then_inc(consts_set, 1)
            pool.memset(power[:, :], -0.5).then_inc(consts_set, 1)
            pool.wait_ge(ident_set, 1)
            pool.affine_select(out=ident[:, :], in_=ident[:, :], compare_op=ALU.not_equal, fill=1.0,
                               base=0, pattern=[[-1, P]], channel_multiplier=1).then_inc(ident_set, 1)
            pool.wait_ge(consts_set, 1)
            pool.affine_select(out=causal[:, :], in_=causal[:, :], compare_op=ALU.is_ge, fill=-FMAX,
                               base=0, pattern=[[-1, P]], channel_multiplier=1).then_inc(consts_set, 1)
            pool.dma_start(gates[:, 0:1], g_xattn.rearrange("(a b) -> a b", a=1)
                           .to_broadcast([P, 1])).then_inc(ld_gate, 16)
            pool.dma_start(gates[:, 1:2], g_ffn.rearrange("(a b) -> a b", a=1)
                           .to_broadcast([P, 1])).then_inc(ld_gate, 16)
            pool.dma_start(gbias[:, 0, :], bo.rearrange("(a b) -> a b", a=1)
                           .to_broadcast([P, P])).then_inc(ld_bias, 16)
            pool.dma_start(gbias[:, 1, :], b_proj.rearrange("(a b) -> a b", a=1)
                           .to_broadcast([P, P])).then_inc(ld_bias, 16)
            pool.dma_start(Afc[:, :], A_fc).then_inc(ld_lora, 16)
            pool.dma_start(Apr[:, :], A_proj).then_inc(ld_lora, 16)
            pool.dma_start(Bfc[:, :, :], B_fc.rearrange("(c p) r -> p c r", p=P)).then_inc(ld_lora, 16)
            pool.dma_start(Bpr[:, :], B_proj).then_inc(ld_lora, 16)
            with nc.allow_non_contiguous_dma(reason="512 biases, once"):
                pool.dma_start(bfc[:, :], b_fc.rearrange("(c p) -> p c", p=P)).then_inc(ld_lora, 16)

            def pair_rstd(i, c):
                pool.wait_ge(ln_stats, 5 * (2 * i + c) + 5)
                mv = meanvar[:, 2 * (c % 2):2 * (c % 2) + 2, 1]
                pool.tensor_tensor(rstd[:, 2 * (c % 2):2 * (c % 2) + 2], mv, power[:, 0:2], ALU.pow)\
                    .then_inc(ln_rstd, 1)

            def pair_resid(i, c):
                pool.wait_ge(ln_done, 2 * i + c + 1)
                xp = X_b[:, bass.ds(4 * i + 2 * c, 2), :]
                pool.tensor_tensor(xp, xp, gbias[:, 0:1, :].to_broadcast([P, 2, P]), ALU.add)\
                    .then_inc(resid_done, 1)

            def normalise(i, c, g):
                pool.wait_ge(inv_done, 16 * i + 2 * c + g + 1)
                pr = prob[:, c % 2, 4 * g:4 * g + 4, :]
                pool.tensor_tensor(pr, pr, invsum[:, c % 2, 4 * g:4 * g + 4].unsqueeze(2)
                                   .to_broadcast([P, 4, P]), ALU.mult).then_inc(prob_done, 1)

            def slot(i, c):
                if exists(i, c - 1):
                    normalise(i, c - 1, 1)
                if c % 4 == 3 and exists(i, c // 4 + 2, PAIRS, 2):
                    pair_rstd(i, c // 4 + 2)
                if exists(i, c):
                    normalise(i, c, 0)
                if c % 4 == 3 and exists(i, c // 4 + 2, PAIRS, 2):
                    pair_resid(i, c // 4 + 2)

            pool.wait_ge(consts_set, 3)
            pair_rstd(0, 0)
            pair_rstd(0, 1)
            pool.wait_ge(wprep, 6)
            pool.partition_all_reduce(wall[:, :], wabs[:, 4:6], P, RMAX).then_inc(wmax_ready, 1)
            pool.wait_ge(gbias_ready, 2)
            pair_resid(0, 0)
            pair_resid(0, 1)
            for c in range(LEAD):
                slot(0, c)
            with pool.Fori(0, STEPS // BODY - 1) as i:
                for c in range(LEAD, LEAD + BODY):
                    slot(i, c)
            for c in range(LEAD, BODY + 1):
                slot(STEPS // BODY - 1, c)

            def group_rstd(i, c):
                pool.wait_ge(f_stats, 5 * (2 * i + c) + 5)
                pool.tensor_tensor(rstd[:, :], meanvar[:, :, 1], power[:, :], ALU.pow)\
                    .then_inc(f_rstd, 1)

            def group_resid(i, c):
                pool.wait_ge(f_norm, 2 * i + c + 1)
                xg = X_b[:, bass.ds(8 * i + 4 * c, 4), :]
                pool.tensor_tensor(xg, xg, gbias[:, 1:2, :].to_broadcast([P, 4, P]), ALU.add)\
                    .then_inc(f_resid, 1)

            with pool.Fori(0, GROUPS // 2) as i:
                for c in range(2):
                    group_rstd(i, c)
                    group_resid(i, c)

        @block.scalar
        def _(act):
            act.dma_start(Wq_sb, Wq).then_inc(ld_wq, 16)
            act.dma_start(X_b[:, 0:FIRST], x_v[:, 0:FIRST]).then_inc(ld_x0, 16)
            act.dma_start(Wv_raw[:, :], Wv).then_inc(ld_wv, 16)
            act.wait_ge(ld_gate, 32)
            act.activation(gates[:, :], gates[:, :], ACT.Tanh).then_inc(gates_ready, 1)
            for n in range(2):
                act.wait_ge(w_turned, n + 1)
                act.activation(WqT[:, 4 * n:4 * n + 4, :],
                               score_bank[n][:, :].rearrange("p (c d) -> p c d", d=P), ACT.Copy)\
                    .then_inc(wqT_ready, 1)
            act.wait_ge(ld_wv, 16)
            act.activation(Wv_hi[:, :], Wv_raw[:, :], ACT.Copy).then_inc(wv_hi_ready, 1)
            for n, bank in enumerate((J0, J1, OB, YB)):
                act.wait_ge(m_ready, n + 1)
                h0 = n % 2 + STEP_HEADS * (n // 2)
                act.activation(M_hi[:, h0:h0 + 7:2, :], bank[:, :].rearrange("p (h d) -> p h d", d=P),
                               ACT.Copy).then_inc(m_hi_ready, 1)

            def job_hi(i, c, n):
                kind, which = JOB[n]
                act.wait_ge(job_done, JOBS * (2 * i + c) + n + 1)
                par, bank = c % 2, job_bank[n % 2]
                if kind == "turn":
                    dst, src = tT_hi[:, par, 2 * P * which:2 * P * which + 2 * P], bank[:, 0:2 * P]
                elif kind == "u":
                    dst = u_hi[:, par, 2 * which:2 * which + 2, :]
                    src = bank[:, :].rearrange("p (h t) -> p h t", h=2)
                else:
                    dst = v[:, par, which // 2, 512 * (which % 2):512 * (which % 2) + 512]
                    src = bank[:, :]
                act.activation(dst, src, ACT.Copy).then_inc(job_hi_done, 1)

            def exps(i, c, g):
                act.wait_ge(negmax_done, 16 * i + 2 * c + g + 1)
                if c >= 2:
                    act.wait_ge(turned_done, 16 * i + 2 * (c - 2) + g + 1)
                for h in range(4 * g, 4 * g + 4):
                    e = act.activation(prob[:, c % 2, h, :], masked[:, c % 2, h, :], ACT.Exp,
                                       bias=negmax[:, c % 2, h:h + 1], scale=SCALE,
                                       accum_out=rowsum[:, c % 2, h:h + 1])
                e.then_inc(exp_done, 1)

            def probT_copy(i, c):
                act.wait_ge(turned_done, 16 * i + 2 * c + 1)
                if c >= 2:
                    act.wait_ge(heads_done, 8 * i + c - 1)
                act.activation(probT[:, c % 2, 0:4, :], T0[:, :].rearrange("p (h j) -> p h j", h=4),
                               ACT.Copy).then_inc(probT0_done, 1)

            def slot(i, c):
                jobs = SLOT_JOBS[c % 4] if exists(i, c // 4 + 1, PAIRS, 2) else []
                pn = c // 4 + 1
                if exists(i, c - 1):
                    exps(i, c - 1, 1)
                for n in jobs[0:2]:
                    job_hi(i, pn, n)
                if exists(i, c - 1):
                    probT_copy(i, c - 1)
                if exists(i, c):
                    exps(i, c, 0)
                for n in jobs[2:]:
                    job_hi(i, pn, n)

            for n in range(JOBS):
                job_hi(0, 0, n)
            act.wait_ge(wm_turned, 1)
            act.activation(W1_hi[:, :], S0[:, :], ACT.Copy).then_inc(w1_hi_ready, 1)
            for c in range(LEAD):
                slot(0, c)
            with act.Fori(0, STEPS // BODY - 1) as i:
                for c in range(LEAD, LEAD + BODY):
                    slot(i, c)
            for c in range(LEAD, LEAD + BODY):
                slot(STEPS // BODY - 1, c)

            def turned_hi(i, c):
                act.wait_ge(f_turned, 2 * i + c + 1)
                act.activation(x2T_hi[:, c % 2], S0[:, :], ACT.Copy).then_inc(f_hi, 1)

            def gelu(i, c, f):
                act.wait_ge(f_up, 4 * (2 * i + c) + f + 1)
                if c >= 2:
                    act.wait_ge(f_down, 2 * i + c - 1)
                act.activation(hid[:, c % 2, f], turn_bank[f % 2][:, :], ACT.Gelu,
                               bias=bfc[:, f:f + 1]).then_inc(f_gelu, 1)

            def group(i, c):
                for f in range(CHUNKS):
                    if exists(i, c, GROUPS, 2):
                        gelu(i, c, f)
                if exists(i, c + 1, GROUPS, 2):
                    turned_hi(i, c + 1)

            act.wait_ge(ld_lora, 80)
            turned_hi(0, 0)
            for c in range(3):
                group(0, c)
            with act.Fori(0, GROUPS // 2 - 2) as i:
                group(i, 3)
                group(i, 4)
            group(GROUPS // 2 - 2, 3)

        @block.vector
        def _(dve):
            def pair_stats(i, c):
                k = 5 * (2 * i + c)
                for r in range(2):
                    dve.bn_stats(stats[:, 2 * (c % 2) + r, :],
                                 X[:, bass.ds((4 * i + 2 * c + r) * P, P)]).then_inc(ln_stats, 1)
                dve.wait_ge(ln_stats, k + 2)
                dve.sem_inc(passed, 1)
                for r in range(2):
                    s = 2 * (c % 2) + r
                    dve.bn_aggr(meanvar[:, s, :], stats[:, s, :]).then_inc(ln_stats, 1)
                dve.wait_ge(ln_stats, k + 4)
                mv = meanvar[:, 2 * (c % 2):2 * (c % 2) + 2, 1]
                dve.tensor_scalar(mv, mv, EPS, None, ALU.add).then_inc(ln_stats, 1)

            def pair_norm(i, c):
                dve.wait_ge(ln_rstd, 2 * i + c + 1)
                for r in range(2):
                    s = 2 * (c % 2) + r
                    n = dve.tensor_scalar(xn[:, c % 2, P * r:P * r + P],
                                          X[:, bass.ds((4 * i + 2 * c + r) * P, P)],
                                          meanvar[:, s, 0:1], rstd[:, s:s + 1],
                                          ALU.subtract, ALU.mult)
                n.then_inc(ln_done, 1)

            def job_lo(i, c, n):
                kind, which = JOB[n]
                if kind == "v":
                    return
                dve.wait_ge(job_hi_done, JOBS * (2 * i + c) + n + 1)
                par, bank = c % 2, job_bank[n % 2]
                if kind == "turn":
                    cut = slice(2 * P * which, 2 * P * which + 2 * P)
                    dst, hi, src = tT_lo[:, par, cut], tT_hi[:, par, cut], bank[:, 0:2 * P]
                else:
                    cut = slice(2 * which, 2 * which + 2)
                    dst, hi = u_lo[:, par, cut, :], u_hi[:, par, cut, :]
                    src = bank[:, :].rearrange("p (h t) -> p h t", h=2)
                dve.tensor_tensor(dst, src, hi.bitcast(F32), ALU.subtract).then_inc(job_lo_done, 1)

            def batch_bias(i, c):
                dve.scalar_tensor_tensor(out=bias[:, c // 2 % 2, :],
                                         in0=maskb[:, bass.ds((4 * i + c // 2) * P, P)], scalar=-FMAX,
                                         in1=causal[:, :], op0=ALU.mult, op1=ALU.min)\
                    .then_inc(bias_done, 1)

            def mask_max(i, c, g):
                if g == 0:
                    dve.wait_ge(bias_done, 4 * i + c // 2 + 1)
                dve.wait_ge(scores_done, 16 * i + 2 * c + g + 1)
                if c >= 2:
                    dve.wait_ge(exp_done, 16 * i + 2 * (c - 2) + g + 1)
                dve.sem_inc(passed, 1)
                for n in range(4):
                    h = 4 * g + n
                    m = dve.tensor_tensor_reduce(masked[:, c % 2, h, :],
                                                 score_bank[g][:, n * P:n * P + P],
                                                 bias[:, c // 2 % 2, :], 1.0, -FMAX, ALU.add, ALU.max,
                                                 rowmax[:, c % 2, h:h + 1])
                m.then_inc(masked_done, 1)
                dve.wait_ge(masked_done, 16 * i + 2 * c + g + 1)
                cut = slice(4 * g, 4 * g + 4)
                dve.tensor_scalar(negmax[:, c % 2, cut], rowmax[:, c % 2, cut], -SCALE, None, ALU.mult)\
                    .then_inc(negmax_done, 1)

            def inverse(i, c, g):
                dve.wait_ge(exp_done, 16 * i + 2 * c + g + 1)
                cut = slice(4 * g, 4 * g + 4)
                dve.reciprocal(invsum[:, c % 2, cut], rowsum[:, c % 2, cut]).then_inc(inv_done, 1)

            def probT_copy(i, c):
                dve.wait_ge(turned_done, 16 * i + 2 * c + 2)
                if c >= 2:
                    dve.wait_ge(heads_done, 8 * i + c - 1)
                dve.tensor_copy(probT[:, c % 2, 4:8, :], T1[:, :].rearrange("p (h j) -> p h j", h=4))\
                    .then_inc(probT1_done, 1)

            def headT_copy(i, c):
                dve.wait_ge(heads_done, 8 * i + c + 1)
                dve.tensor_copy(headT[:, c % 2, :], OB[:, :]).then_inc(headT_done, 1)

            def add_y(i, c):
                dve.wait_ge(y_done, 8 * i + c + 1)
                dve.wait_ge(resid_done, 2 * i + c // 4 + 1)
                xb = X[:, bass.ds((4 * i + c // 2) * P, P)]
                dve.tensor_tensor(xb, YB[:, 0:P], xb, ALU.add).then_inc(x_done, 1)

            def slot(i, c):
                jobs = SLOT_JOBS[c % 4] if exists(i, c // 4 + 1, PAIRS, 2) else []
                pn = c // 4 + 1
                ln = c % 4 == 3 and exists(i, c // 4 + 2, PAIRS, 2)
                if exists(i, c) and c % 2 == 0:
                    batch_bias(i, c)
                if c >= 1 and exists(i, (c - 1) // 4 + 1, PAIRS, 2):
                    for n in SLOT_JOBS[(c - 1) % 4][2:]:
                        job_lo(i, (c - 1) // 4 + 1, n)
                if exists(i, c):
                    mask_max(i, c, 0)
                if exists(i, c - 1):
                    inverse(i, c - 1, 1)
                if exists(i, c):
                    mask_max(i, c, 1)
                for n in jobs[0:1]:
                    job_lo(i, pn, n)
                if exists(i, c - 2):
                    headT_copy(i, c - 2)
                if exists(i, c - 1):
                    probT_copy(i, c - 1)
                for n in jobs[1:2]:
                    job_lo(i, pn, n)
                if exists(i, c - 3) and c % 2 == 0:
                    add_y(i, c - 3)
                if ln:
                    pair_stats(i, c // 4 + 2)
                if exists(i, c):
                    inverse(i, c, 0)
                if ln:
                    pair_norm(i, c // 4 + 2)

            dve.wait_ge(ld_x0, 16)
            pair_stats(0, 0)
            for n in range(2):
                dve.wait_ge(w_turned, n + 3)
                dve.tensor_copy(WkT[:, 4 * n:4 * n + 4, :],
                                turn_bank[n][:, :].rearrange("p (c d) -> p c d", d=P))\
                    .then_inc(wkT_ready, 1)
            pair_norm(0, 0)
            pair_stats(0, 1)
            for n, bank in enumerate((J0, J1, OB, YB)):
                dve.wait_ge(m_hi_ready, n + 1)
                cut = slice(n % 2 + STEP_HEADS * (n // 2), n % 2 + STEP_HEADS * (n // 2) + 7, 2)
                dve.tensor_tensor(M_lo[:, cut, :], bank[:, :].rearrange("p (h d) -> p h d", d=P),
                                  M_hi[:, cut, :].bitcast(F32), ALU.subtract).then_inc(m_lo_ready, 1)
            dve.wait_ge(wv_hi_ready, 1)
            dve.tensor_tensor(Wv_lo[:, :], Wv_raw[:, :], Wv_hi[:, :].bitcast(F32), ALU.subtract)\
                .then_inc(wv_lo_ready, 1)
            pair_norm(0, 1)
            dve.wait_ge(gates_ready, 1)
            dve.wait_ge(ld_bias, 32)
            for n in range(2):
                dve.tensor_scalar(gbias[:, n, :], gbias[:, n, :], gates[:, n:n + 1], None, ALU.mult)\
                    .then_inc(gbias_ready, 1)
            dve.wait_ge(ld_wo, 16)
            dve.tensor_scalar(Wo_sb[:, :, :], Wo_sb[:, :, :], gates[:, 0:1], None, ALU.mult)\
                .then_inc(wo_ready, 1)
            dve.wait_ge(ld_ffn, 32)
            for n in range(2):
                dve.tensor_reduce(wabs[:, n:n + 1], Wf[:, n, :], AX.X, ALU.max).then_inc(wprep, 1)
                dve.tensor_reduce(wabs[:, 2 + n:3 + n], Wf[:, n, :], AX.X, ALU.min).then_inc(wprep, 1)
            dve.wait_ge(wprep, 4)
            for n in range(2):
                dve.scalar_tensor_tensor(out=wabs[:, 4 + n:5 + n], in0=wabs[:, 2 + n:3 + n], scalar=-1.0,
                                         in1=wabs[:, n:n + 1], op0=ALU.mult, op1=ALU.max)\
                    .then_inc(wprep, 1)
            for n in range(JOBS):
                job_lo(0, 0, n)
            dve.wait_ge(bT_turned, 1)
            dve.tensor_copy(BT[:, 0:FF], S0[0:RANK, :]).then_inc(bT_ready, 1)
            dve.tensor_copy(BT[:, FF:FF + P], S1[0:RANK, 0:P]).then_inc(bT_ready, 1)
            dve.wait_ge(wmax_ready, 1)
            dve.tensor_scalar(wscale[:, 0:2], wall[:, :], 1.0 / QMAX, None, ALU.mult).then_inc(wprep, 1)
            dve.wait_ge(wprep, 7)
            dve.reciprocal(wscale[:, 2:4], wscale[:, 0:2]).then_inc(wprep, 1)
            for n in range(2):
                dve.wait_ge(wprep, 8 + 3 * n)
                dve.tensor_scalar(Wt[:, n, :], Wf[:, n, :], wscale[:, 2 + n:3 + n], ROUND,
                                  ALU.mult, ALU.add).then_inc(wprep, 1)
                dve.wait_ge(wprep, 9 + 3 * n)
                dve.tensor_scalar(Wt[:, n, :], Wt[:, n, :], ROUND, QMAX, ALU.subtract, ALU.min)\
                    .then_inc(wprep, 1)
                dve.wait_ge(wprep, 10 + 3 * n)
                dve.tensor_scalar(Wt[:, n, :], Wt[:, n, :], -QMAX - 1, wscale[:, n:n + 1],
                                  ALU.max, ALU.mult).then_inc(wprep, 1)
            dve.wait_ge(lora_ready, 1)
            dve.wait_ge(wprep, 14)
            for n in range(2):
                dve.scalar_tensor_tensor(out=Wt[:, n, :], in0=turn_bank[n][:, :], scalar=LORA_SCALE,
                                         in1=Wt[:, n, :], op0=ALU.mult, op1=ALU.add).then_inc(wprep, 1)
            dve.wait_ge(w1_hi_ready, 1)
            dve.tensor_tensor(W1_lo[:, :], S0[:, :], W1_hi[:, :].bitcast(F32), ALU.subtract)\
                .then_inc(w12_ready, 1)
            dve.tensor_scalar(W2T[:, :, :], S1[:, :].rearrange("p (c d) -> p c d", d=P), gates[:, 1:2],
                              None, ALU.mult).then_inc(w12_ready, 1)
            dve.wait_ge(ld_mask, 16)
            dve.wait_ge(consts_set, 3)
            for c in range(LEAD):
                slot(0, c)
            dve.wait_ge(ld_x1, 16)
            with dve.Fori(0, STEPS // BODY - 1) as i:
                for c in range(LEAD, LEAD + BODY):
                    slot(i, c)
            for c in range(LEAD, LEAD + BODY):
                slot(STEPS // BODY - 1, c)

            def group_stats(i, c):
                k = 5 * (2 * i + c)
                for b in range(4):
                    s = dve.bn_stats(stats[:, b, :], X[:, bass.ds((8 * i + 4 * c + b) * P, P)])
                    s.then_inc(f_stats, 1) if b in (1, 3) else None
                dve.wait_ge(f_stats, k + 2)
                dve.sem_inc(passed, 1)
                for b in range(4):
                    s = dve.bn_aggr(meanvar[:, b, :], stats[:, b, :])
                    s.then_inc(f_stats, 1) if b in (1, 3) else None
                dve.wait_ge(f_stats, k + 4)
                dve.tensor_scalar(meanvar[:, :, 1], meanvar[:, :, 1], EPS, None, ALU.add)\
                    .then_inc(f_stats, 1)

            def group_norm(i, c):
                dve.wait_ge(f_rstd, 2 * i + c + 1)
                if c >= 2:
                    dve.wait_ge(f_turned, 2 * i + c - 1)
                for b in range(4):
                    n = dve.tensor_scalar(xn2[:, c % 2, b * P:b * P + P],
                                          X[:, bass.ds((8 * i + 4 * c + b) * P, P)],
                                          meanvar[:, b, 0:1], rstd[:, b:b + 1],
                                          ALU.subtract, ALU.mult)
                n.then_inc(f_norm, 1)

            def turned_lo(i, c):
                dve.wait_ge(f_hi, 2 * i + c + 1)
                dve.tensor_tensor(x2T_lo[:, c % 2], S0[:, :], x2T_hi[:, c % 2].bitcast(F32),
                                  ALU.subtract).then_inc(f_lo, 1)

            def group_out(i, c):
                dve.wait_ge(f_down, 2 * i + c + 1)
                dve.wait_ge(f_resid, 2 * i + c + 1)
                if c >= 2:
                    dve.wait_ge(stored[c % 2], 16 * (i + c // 2))
                dve.tensor_tensor(yout[:, c % 2], job_bank[c % 2][:, :],
                                  X[:, bass.ds((8 * i + 4 * c) * P, 4 * P)], ALU.add)\
                    .then_inc(f_out, 1)

            def group(i, c):
                if exists(i, c + 1, GROUPS, 2):
                    group_stats(i, c + 1)
                    group_norm(i, c + 1)
                if exists(i, c - 1, GROUPS, 2):
                    group_out(i, c - 1)
                if exists(i, c + 1, GROUPS, 2):
                    turned_lo(i, c + 1)

            dve.wait_ge(x_done, BATCHES)
            group_stats(0, 0)
            group_norm(0, 0)
            turned_lo(0, 0)
            for c in range(3):
                group(0, c)
            with dve.Fori(0, GROUPS // 2 - 2) as i:
                group(i, 3)
                group(i, 4)
            group(GROUPS // 2 - 2, 3)
            group(GROUPS // 2 - 2, 4)

        @block.tensor
        def _(pe):
            def split3(dst, w_hi, w_lo, m_hi, m_lo):
                pe.matmul(dst, w_hi, m_hi, start=True, stop=False)
                pe.matmul(dst, w_hi, m_lo, start=False, stop=False)
                return pe.matmul(dst, w_lo, m_hi, start=False, stop=True)

            pe.wait_ge(ident_set, 2)
            for w, loaded, banks in ((Wq_sb, ld_wq, score_bank), (Wk_sb, ld_wk, turn_bank)):
                pe.wait_ge(loaded, 16)
                for n in range(2):
                    for c in range(4):
                        t = pe.transpose(banks[n][:, c * P:c * P + P],
                                         w[:, (4 * n + c) * P:(4 * n + c + 1) * P], ident[:, :])
                    t.then_inc(w_turned, 1)
            pe.wait_ge(wqT_ready, 2)
            pe.wait_ge(wkT_ready, 2)
            for n, bank in enumerate((J0, J1, OB, YB)):
                rows = slice(DH * (n % 2), DH * (n % 2) + DH)
                for k in range(4):
                    ch = 4 * (n // 2) + k
                    m = pe.matmul(bank[:, k * P:k * P + P], WkT[rows, ch, :], WqT[rows, ch, :],
                                  start=True, stop=True)
                m.then_inc(m_ready, 1)

            def job(i, c, n):
                kind, which = JOB[n]
                par, bank = c % 2, job_bank[n % 2]
                pair = 2 * i + c
                if n >= 2 or c >= 1:
                    last = JOBS * pair + n - 2
                    pe.wait_ge(job_hi_done, last + 1)
                    if JOB[n - 2][0] != "v":
                        pe.wait_ge(job_lo_done, NSPLIT * pair + (
                            splits_before(n - 1) if n >= 2 else splits_before(JOBS + n - 1) - NSPLIT))
                if kind == "turn":
                    if which == 0:
                        pe.wait_ge(ln_done, pair + 1)
                    else:
                        pe.wait_ge((ld_c0, ld_c1)[par], 16 * (i + c // 2 + 1))
                    for r in range(2):
                        m = pe.transpose(bank[:, r * P:r * P + P],
                                         (xn, C)[which][:, par, r * P:r * P + P], ident[:, :])
                elif kind == "u":
                    pe.wait_ge(job_lo_done, NSPLIT * pair + 2)
                    for r in range(2):
                        h = 2 * which + r
                        m = split3(bank[:, 256 * r:256 * r + 256], M_hi[:, h, :], M_lo[:, h, :],
                                   tT_hi[:, par, 2 * P:4 * P], tT_lo[:, par, 2 * P:4 * P])
                else:
                    cols = slice(512 * (which % 2), 512 * (which % 2) + 512)
                    keys = slice((2 + which // 2) * P, (3 + which // 2) * P)
                    m = split3(bank[:, :], tT_hi[:, par, keys], tT_lo[:, par, keys],
                               Wv_hi[:, cols], Wv_lo[:, cols])
                m.then_inc(job_done, 1)

            def scores(i, c):
                r, half = c // 2 % 2, c % 2
                par = c // 4 % 2
                pair = 2 * i + c // 4
                pe.wait_ge(job_lo_done,
                           NSPLIT * pair + splits_before(JOB.index(("u", 4 * half + 3)) + 1))
                for g in range(2):
                    if c >= 1:
                        pe.wait_ge(masked_done, 16 * i + 2 * (c - 1) + g + 1)
                    hs = slice(8 * half + 4 * g, 8 * half + 4 * g + 4)
                    split3(score_bank[g][:, :].rearrange("p (h j) -> p h j", h=4),
                           tT_hi[:, par, r * P:r * P + P], tT_lo[:, par, r * P:r * P + P],
                           u_hi[:, par, hs, r * P:r * P + P], u_lo[:, par, hs, r * P:r * P + P])\
                        .then_inc(scores_done, 1)

            def turn(i, c):
                for g in range(2):
                    pe.wait_ge(prob_done, 16 * i + 2 * c + g + 1)
                    if c >= 1:
                        pe.wait_ge((probT0_done, probT1_done)[g], 8 * i + c)
                    for n in range(4):
                        t = pe.transpose(turn_bank[g][:, n * P:n * P + P],
                                         prob[:, c % 2, 4 * g + n, :], ident[:, :])
                    t.then_inc(turned_done, 1)

            def attend(i, c):
                par, r, half = c // 4 % 2, c // 2 % 2, c % 2
                pe.wait_ge(job_hi_done, JOBS * (2 * i + c // 4) + JOB.index(("v", 2 * r + 1)) + 1)
                if c >= 1:
                    pe.wait_ge(headT_done, 8 * i + c)
                pe.wait_ge(probT0_done, 8 * i + c + 1)
                for h in range(STEP_HEADS):
                    if h == 4:
                        pe.wait_ge(probT1_done, 8 * i + c + 1)
                    rows = slice(DH * (h % 2), DH * (h % 2) + DH)
                    col = (8 * half + h) * DH
                    m = pe.matmul(OB[rows, h // 2 * P:h // 2 * P + P], v[:, par, r, col:col + DH],
                                  probT[:, c % 2, h, :], start=True, stop=True)
                m.then_inc(heads_done, 1)

            def project(i, c):
                half = c % 2
                if half == 0 and c >= 2:
                    pe.wait_ge(x_done, 4 * i + c // 2)
                pe.wait_ge(headT_done, 8 * i + c + 1)
                for q in range(4):
                    m = pe.matmul(YB[:, 0:P], headT[:, c % 2, q * P:q * P + P],
                                  Wo_sb[:, 4 * half + q, :], start=(half == 0 and q == 0),
                                  stop=(half == 1 and q == 3))
                m.then_inc(y_done, 1)

            def slot(i, c):
                jobs = SLOT_JOBS[c % 4] if exists(i, c // 4 + 1, PAIRS, 2) else []
                pn = c // 4 + 1
                if exists(i, c):
                    scores(i, c)
                for n in jobs[0:2]:
                    job(i, pn, n)
                if exists(i, c - 1):
                    turn(i, c - 1)
                for n in jobs[2:3]:
                    job(i, pn, n)
                if exists(i, c - 1):
                    attend(i, c - 1)
                for n in jobs[3:]:
                    job(i, pn, n)
                if exists(i, c - 2):
                    project(i, c - 2)

            pe.wait_ge(m_lo_ready, 4)
            pe.wait_ge(wv_lo_ready, 1)
            for n in range(JOBS):
                job(0, 0, n)
            pe.wait_ge(ld_lora, 80)
            for c in range(CHUNKS):
                pe.transpose(S0[0:RANK, c * P:c * P + P], Bfc[:, c, :], ident[:, :])
            pe.transpose(S1[0:RANK, 0:P], Bpr[:, :], ident[:, :]).then_inc(bT_turned, 1)
            pe.wait_ge(bT_ready, 2)
            for c in range(CHUNKS):
                pe.matmul(T0[:, c * P:c * P + P], BT[:, c * P:c * P + P], Afc[:, :],
                          start=True, stop=True)
            pe.matmul(T1[:, :], BT[:, FF:FF + P], Apr[:, :], start=True, stop=True)\
                .then_inc(lora_ready, 1)
            pe.wait_ge(wprep, 16)
            for n in range(2):
                for c in range(CHUNKS):
                    t = pe.transpose(score_bank[n][:, c * P:c * P + P], Wt[:, n, c * P:c * P + P],
                                     ident[:, :])
            t.then_inc(wm_turned, 1)
            pe.wait_ge(w12_ready, 2)
            pe.wait_ge(wo_ready, 1)
            for c in range(LEAD):
                slot(0, c)
            with pe.Fori(0, STEPS // BODY - 1) as i:
                for c in range(LEAD, LEAD + BODY):
                    slot(i, c)
            for c in range(LEAD, LEAD + BODY):
                slot(STEPS // BODY - 1, c)

            def turn_x(i, c):
                pe.wait_ge(f_norm, 2 * i + c + 1)
                if c >= 1:
                    pe.wait_ge(f_lo, 2 * i + c)
                for b in range(4):
                    t = pe.transpose(S0[:, b * P:b * P + P], xn2[:, c % 2, b * P:b * P + P],
                                     ident[:, :])
                t.then_inc(f_turned, 1)

            def up(i, c, f):
                pe.wait_ge(f_lo, 2 * i + c + 1)
                if c >= 1 or f >= 2:
                    pe.wait_ge(f_gelu, 4 * (2 * i + c) + f - 1)
                split3(turn_bank[f % 2][:, :], W1_hi[:, f * P:f * P + P], W1_lo[:, f * P:f * P + P],
                       x2T_hi[:, c % 2], x2T_lo[:, c % 2]).then_inc(f_up, 1)

            def down(i, c, t):
                pe.wait_ge(f_gelu, 4 * (2 * i + c) + 4)
                if c >= 2:
                    pe.wait_ge(f_out, 2 * i + c - 1)
                for f in range(CHUNKS):
                    m = pe.matmul(job_bank[c % 2][:, t * P:t * P + P],
                                  hid[:, c % 2, f, t * P:t * P + P], W2T[:, f, :],
                                  start=(f == 0), stop=(f == CHUNKS - 1))
                if t == 3:
                    m.then_inc(f_down, 1)

            def group(i, c):
                for f in range(CHUNKS):
                    if exists(i, c, GROUPS, 2):
                        up(i, c, f)
                    if exists(i, c - 1, GROUPS, 2):
                        down(i, c - 1, f)
                if exists(i, c + 1, GROUPS, 2):
                    turn_x(i, c + 1)

            turn_x(0, 0)
            for c in range(3):
                group(0, c)
            with pe.Fori(0, GROUPS // 2 - 2) as i:
                group(i, 3)
                group(i, 4)
            group(GROUPS // 2 - 2, 3)
            group(GROUPS // 2 - 2, 4)


_INS = ["x", "ctx_1024", "mask_BxS2_bf0", "g_xattn", "g_ffn", "L0_xattn_Wq", "L0_xattn_Wk",
        "L0_xattn_Wv", "L0_xattn_Wo", "L0_xattn_bo", "L0_ffn_W_fc", "L0_ffn_b_fc", "L0_ffn_A_fc",
        "L0_ffn_B_fc", "L0_ffn_W_proj", "L0_ffn_b_proj", "L0_ffn_A_proj", "L0_ffn_B_proj"]


def kernel(**inputs):
    import concourse.bacc as bacc
    from concourse.bass_utils import run_bass_kernel_spmd

    nc = bacc.Bacc("TRN2", target_bir_lowering=False, num_devices=1)
    arrays, args = {}, []
    for name in _INS:
        a = np.ascontiguousarray(inputs[name])
        arrays[f"in_{name}"] = a
        args.append(nc.dram_tensor(f"in_{name}", a.shape, mybir.dt.from_np(a.dtype),
                                   kind="ExternalInput").ap())
    args.append(nc.dram_tensor("out", (BATCHES, P, P), F32, kind="ExternalOutput").ap())
    build(nc, *args)
    r = run_bass_kernel_spmd(nc, [arrays], core_ids=[0])
    return r.results[0]["out"]
```

```python
from contextlib import ExitStack

import concourse.bass as bass
import concourse.mybir as mybir
import numpy as np

F32 = mybir.dt.float32
F32R = mybir.dt.float32r
ALU = mybir.AluOpType
ACT = mybir.ActivationFunctionType
AX = mybir.AxisListType
RMAX = bass.bass_isa.ReduceOp.max

P = 128
BATCHES, HEADS, DH = 32, 16, 64
INNER = HEADS * DH
FF, RANK = 512, 16
CHUNKS = FF // P
SCALE = DH ** -0.5
EPS = 1e-5
FMAX = float(np.finfo(np.float32).max)
QMAX = 127.0
LORA_SCALE = 2.0
ROUND = 12582912.0

PAIRS = BATCHES // 2
STEP_HEADS = 8
STEPS = BATCHES * HEADS // STEP_HEADS
BODY = 8
LEAD = 3
JOBS = 14
JOB = [("turn", 1), ("turn", 0), ("u", 0), ("u", 1), ("v", 0), ("u", 2), ("u", 3), ("v", 1),
       ("u", 4), ("u", 5), ("v", 2), ("u", 6), ("u", 7), ("v", 3)]
SPLITS = [n for n, (kind, _) in enumerate(JOB) if kind != "v"]
NSPLIT = len(SPLITS)
GROUPS = BATCHES // 4


def splits_before(n):
    return sum(m < n for m in SPLITS)


def slot_jobs(i, c):
    jobs = []
    if exists(i, c // 4 + 1, PAIRS, 2):
        jobs += [(c // 4 + 1, 2 + 3 * (c % 4) + m) for m in range(3)]
    if c % 4 == 3 and exists(i, c // 4 + 2, PAIRS, 2):
        jobs += [(c // 4 + 2, 0), (c // 4 + 2, 1)]
    return jobs


def exists(i, c, end=STEPS, per=BODY):
    return not isinstance(i, int) or 0 <= per * i + c < end


def build(nc, x, ctx, mask, g_xattn, g_ffn, Wq, Wk, Wv, Wo, bo, W_fc, b_fc, A_fc, B_fc, W_proj,
          b_proj, A_proj, B_proj, out):
    st = ExitStack()
    with st:
        def sb(name, shape, dt=F32):
            return st.enter_context(nc.sbuf_tensor(name, shape, dt))

        def sem(name):
            return st.enter_context(nc.semaphore(name))

        X = sb("X", [P, BATCHES * P])
        C = sb("C", [P, 2, 2 * P])
        maskb = sb("maskb", [P, BATCHES * P], mybir.dt.uint8)
        ident = sb("ident", [P, P])
        causal = sb("causal", [P, P])
        bias = sb("bias", [P, 2, P])
        xn = sb("xn", [P, 2, 2 * P])
        tT_hi = sb("tT_hi", [P, 2, 4 * P], F32R)
        tT_lo = sb("tT_lo", [P, 2, 4 * P], F32R)
        u_hi = sb("u_hi", [P, 2, HEADS, 2 * P], F32R)
        u_lo = sb("u_lo", [P, 2, HEADS, 2 * P], F32R)
        v = sb("v", [P, 2, 2, INNER])
        masked = sb("masked", [P, 2, STEP_HEADS, P])
        prob = sb("prob", [P, 2, STEP_HEADS, P])
        probT = sb("probT", [P, 2, STEP_HEADS, P])
        headT = sb("headT", [P, 2, 4 * P])
        rowmax = sb("rowmax", [P, 2, STEP_HEADS])
        negmax = sb("negmax", [P, 2, STEP_HEADS])
        rowsum = sb("rowsum", [P, 2, STEP_HEADS])
        invsum = sb("invsum", [P, 2, STEP_HEADS])
        stats = sb("stats", [P, 4, 6])
        meanvar = sb("meanvar", [P, 4, 2])
        rstd = sb("rstd", [P, 4])
        power = sb("power", [P, 4])
        M_hi = sb("M_hi", [P, HEADS, P], F32R)
        M_lo = sb("M_lo", [P, HEADS, P], F32R)
        Wv_raw = sb("Wv_raw", [P, INNER])
        Wv_hi = sb("Wv_hi", [P, INNER], F32R)
        Wv_lo = sb("Wv_lo", [P, INNER], F32R)
        Wo_sb = sb("Wo_sb", [P, INNER // P, P])
        gates = sb("gates", [P, 2])
        gbias = sb("gbias", [P, 2, P])
        Wf = sb("Wf", [P, 2, FF])
        Wt = sb("Wt", [P, 2, FF])
        W1_hi = sb("W1_hi", [P, FF], F32R)
        W1_lo = sb("W1_lo", [P, FF], F32R)
        W2T = sb("W2T", [P, CHUNKS, P])
        bfc = sb("bfc", [P, CHUNKS])
        Afc = sb("Afc", [RANK, P])
        Apr = sb("Apr", [RANK, FF])
        Bfc = sb("Bfc", [P, CHUNKS, RANK])
        Bpr = sb("Bpr", [P, RANK])
        BT = sb("BT", [RANK, FF + P])
        wabs = sb("wabs", [P, 6])
        wall = sb("wall", [P, 2])
        wscale = sb("wscale", [P, 4])
        Wq_sb, Wk_sb = (probT[:, n].rearrange("p h j -> p (h j)") for n in range(2))
        WqT, WkT = (prob[:, n] for n in range(2))
        hid = v[:, :].rearrange("p a b (f t) -> p a (b f) t", f=2)
        xn2 = (xn[:, :].rearrange("p a t -> p (a t)"), C[:, :].rearrange("p a t -> p (a t)"))
        x2T_hi = u_hi[:, 0, 0:4].rearrange("p (a b) t -> p a (b t)", a=2)
        x2T_lo = u_lo[:, 0, 0:4].rearrange("p (a b) t -> p a (b t)", a=2)

        S0, S1, T0, T1, J0, J1, OB, YB = (
            st.enter_context(nc.psum_tensor(n, [P, 512], F32))
            for n in ("S0", "S1", "T0", "T1", "J0", "J1", "OB", "YB"))
        score_bank, turn_bank, job_bank = (S0, S1), (T0, T1), (J0, J1)
        first_job_bank = (J0, J1, T0, T1, S0, S1)

        def bank_of(pair, n):
            return first_job_bank[n % 6] if pair == 0 else job_bank[n % 2]

        M_BANKS = (OB, YB, S0, S1)

        (ld_wq, ld_wk, ld_x0, ld_c0, ld_x1, ld_c1, ld_mask, ld_wv, ld_wo, ld_bias, ld_gate, ld_ffn,
         ld_lora) = (sem(n) for n in (
             "ld_wq", "ld_wk", "ld_x0", "ld_c0", "ld_x1", "ld_c1", "ld_mask", "ld_wv", "ld_wo",
             "ld_bias", "ld_gate", "ld_ffn", "ld_lora"))
        (ident_set, consts_set, w_turned, wqT_ready, wkT_ready, m_ready, m_hi_ready, m_lo_ready,
         wv_hi_ready, wv_lo_ready, gates_ready, wo_ready, gbias_ready, bT_turned, bT_ready,
         lora_ready, wprep, wmax_ready, wm_turned, w1_hi_ready, w12_ready) = (sem(n) for n in (
             "ident_set", "consts_set", "w_turned", "wqT_ready", "wkT_ready", "m_ready",
             "m_hi_ready", "m_lo_ready", "wv_hi_ready", "wv_lo_ready", "gates_ready", "wo_ready",
             "gbias_ready", "bT_turned", "bT_ready", "lora_ready", "wprep", "wmax_ready",
             "wm_turned", "w1_hi_ready", "w12_ready"))
        (scores_done, masked_done, negmax_done, exp_done, inv_done, prob_done, turned_done,
         probT0_done, probT1_done, heads_done, headT_done, y_done, x_done, bias_done, job_done,
         job_hi_done, job_lo_done, ln_stats, ln_rstd, ln_done, resid_done) = (sem(n) for n in (
             "scores_done", "masked_done", "negmax_done", "exp_done", "inv_done", "prob_done",
             "turned_done", "probT0_done", "probT1_done", "heads_done", "headT_done", "y_done",
             "x_done", "bias_done", "job_done", "job_hi_done", "job_lo_done", "ln_stats", "ln_rstd",
             "ln_done", "resid_done"))
        (f_stats, f_rstd, f_norm, f_turned, f_hi, f_lo, f_up, f_gelu, f_down, f_out, f_resid,
         stored) = (sem(n) for n in (
             "f_stats", "f_rstd", "f_norm", "f_turned", "f_hi", "f_lo", "f_up", "f_gelu", "f_down",
             "f_out", "f_resid", "stored"))
        passed = sem("passed")

        block = st.enter_context(nc.Block())

        x_v = x.rearrange("b p d -> p b d")
        c_v = ctx.rearrange("b p d -> p b d")
        out_v = out.rearrange("b p d -> p b d")
        X_b = X[:, :].rearrange("p (b d) -> p b d", d=P)
        FIRST = 4

        @block.sync
        def _(sp):
            sp.dma_start(Wk_sb, Wk).then_inc(ld_wk, 16)

            def load_ctx(i, c):
                if c >= 2:
                    sp.wait_ge(job_done, JOBS * (2 * i + c - 2) + 1)
                sp.dma_start(C[:, c % 2, :].rearrange("p (b d) -> p b d", d=P),
                             c_v[:, bass.ds(4 * i + 2 * c, 2), :]).then_inc((ld_c0, ld_c1)[c % 2], 16)

            load_ctx(0, 0)
            load_ctx(0, 1)
            sp.dma_start(maskb[:, :], mask.rearrange("(a b) j -> a (b j)", a=1)
                         .to_broadcast([P, BATCHES * P])).then_inc(ld_mask, 16)
            sp.dma_start(Wo_sb[:, :, :], Wo.rearrange("(q p) d -> p q d", p=P)).then_inc(ld_wo, 16)
            sp.dma_start(X_b[:, FIRST:BATCHES], x_v[:, FIRST:BATCHES]).then_inc(ld_x1, 16)
            sp.dma_start(Wf[:, 0, :].rearrange("p (c d) -> p c d", d=P),
                         W_fc.rearrange("(c p) d -> p c d", p=P)).then_inc(ld_ffn, 16)
            sp.dma_start(Wf[:, 1, :], W_proj).then_inc(ld_ffn, 16)

            with sp.Fori(0, PAIRS // 2 - 1) as i:
                load_ctx(i, 2)
                load_ctx(i, 3)

            with sp.Fori(0, GROUPS) as i:
                sp.wait_ge(f_out, i + 1)
                sp.dma_start(out_v[:, bass.ds(4 * i, 4), :],
                             X_b[:, bass.ds(4 * i, 4), :]).then_inc(stored, 16)
            sp.wait_ge(stored, 16 * GROUPS)

        @block.gpsimd
        def _(pool):
            pool.memset(ident[:, :], 0.0).then_inc(ident_set, 1)
            pool.memset(causal[:, :], 0.0).then_inc(consts_set, 1)
            pool.memset(power[:, :], -0.5).then_inc(consts_set, 1)
            pool.wait_ge(ident_set, 1)
            pool.affine_select(out=ident[:, :], in_=ident[:, :], compare_op=ALU.not_equal, fill=1.0,
                               base=0, pattern=[[-1, P]], channel_multiplier=1).then_inc(ident_set, 1)
            pool.wait_ge(consts_set, 1)
            pool.affine_select(out=causal[:, :], in_=causal[:, :], compare_op=ALU.is_ge, fill=-FMAX,
                               base=0, pattern=[[-1, P]], channel_multiplier=1).then_inc(consts_set, 1)
            pool.wait_ge(consts_set, 2)

            def pair_rstd(i, c):
                pool.wait_ge(ln_stats, 5 * (2 * i + c) + 5)
                mv = meanvar[:, 2 * (c % 2):2 * (c % 2) + 2, 1]
                pool.tensor_tensor(rstd[:, 2 * (c % 2):2 * (c % 2) + 2], mv, power[:, 0:2], ALU.pow)\
                    .then_inc(ln_rstd, 1)

            pair_rstd(0, 0)
            pool.dma_start(gates[:, 0:1], g_xattn.rearrange("(a b) -> a b", a=1)
                           .to_broadcast([P, 1])).then_inc(ld_gate, 16)
            pool.dma_start(gates[:, 1:2], g_ffn.rearrange("(a b) -> a b", a=1)
                           .to_broadcast([P, 1])).then_inc(ld_gate, 16)
            pool.dma_start(gbias[:, 0, :], bo.rearrange("(a b) -> a b", a=1)
                           .to_broadcast([P, P])).then_inc(ld_bias, 16)
            pool.dma_start(gbias[:, 1, :], b_proj.rearrange("(a b) -> a b", a=1)
                           .to_broadcast([P, P])).then_inc(ld_bias, 16)
            pool.dma_start(Afc[:, :], A_fc).then_inc(ld_lora, 16)
            pool.dma_start(Apr[:, :], A_proj).then_inc(ld_lora, 16)
            pool.dma_start(Bfc[:, :, :], B_fc.rearrange("(c p) r -> p c r", p=P)).then_inc(ld_lora, 16)
            pool.dma_start(Bpr[:, :], B_proj).then_inc(ld_lora, 16)
            with nc.allow_non_contiguous_dma(reason="512 biases, once"):
                pool.dma_start(bfc[:, :], b_fc.rearrange("(c p) -> p c", p=P)).then_inc(ld_lora, 16)

            def pair_resid(i, c):
                pool.wait_ge(ln_done, 2 * i + c + 1)
                xp = X_b[:, bass.ds(4 * i + 2 * c, 2), :]
                pool.tensor_tensor(xp, xp, gbias[:, 0:1, :].to_broadcast([P, 2, P]), ALU.add)\
                    .then_inc(resid_done, 1)

            def normalise(i, c, g):
                pool.wait_ge(inv_done, 16 * i + 2 * c + g + 1)
                pr = prob[:, c % 2, 4 * g:4 * g + 4, :]
                pool.tensor_tensor(pr, pr, invsum[:, c % 2, 4 * g:4 * g + 4].unsqueeze(2)
                                   .to_broadcast([P, 4, P]), ALU.mult).then_inc(prob_done, 1)

            def slot(i, c):
                if exists(i, c - 1):
                    normalise(i, c - 1, 1)
                if c % 4 == 3 and exists(i, c // 4 + 2, PAIRS, 2):
                    pair_rstd(i, c // 4 + 2)
                if exists(i, c):
                    normalise(i, c, 0)
                if c % 4 == 3 and exists(i, c // 4 + 2, PAIRS, 2):
                    pair_resid(i, c // 4 + 2)

            pair_rstd(0, 1)
            pool.wait_ge(wv_hi_ready, 1)
            pool.tensor_tensor(Wv_lo[:, :], Wv_raw[:, :], Wv_hi[:, :].bitcast(F32), ALU.subtract)\
                .then_inc(wv_lo_ready, 1)
            pool.wait_ge(gbias_ready, 2)
            pair_resid(0, 0)
            pair_resid(0, 1)
            for c in range(LEAD):
                slot(0, c)
            with pool.Fori(0, STEPS // BODY - 1) as i:
                for c in range(LEAD, LEAD + BODY):
                    slot(i, c)

            def group_rstd(i, c):
                pool.wait_ge(f_stats, 5 * (2 * i + c) + 5)
                pool.tensor_tensor(rstd[:, :], meanvar[:, :, 1], power[:, :], ALU.pow)\
                    .then_inc(f_rstd, 1)

            def group_resid(i, c):
                pool.wait_ge(f_norm, 2 * i + c + 1)
                xg = X_b[:, bass.ds(8 * i + 4 * c, 4), :]
                pool.tensor_tensor(xg, xg, gbias[:, 1:2, :].to_broadcast([P, 4, P]), ALU.add)\
                    .then_inc(f_resid, 1)

            for c in range(LEAD, BODY + 1):
                slot(STEPS // BODY - 1, c)
                if c == 4:
                    pool.wait_ge(wprep, 6)
                    pool.partition_all_reduce(wall[:, :], wabs[:, 4:6], P, RMAX).then_inc(wmax_ready, 1)
                if c == 6:
                    group_rstd(0, 0)
            group_resid(0, 0)
            group_rstd(0, 1)
            group_resid(0, 1)
            with pool.Fori(1, GROUPS // 2) as i:
                for c in range(2):
                    group_rstd(i, c)
                    group_resid(i, c)

        @block.scalar
        def _(act):
            act.dma_start(Wq_sb, Wq).then_inc(ld_wq, 16)
            act.dma_start(X_b[:, 0:FIRST], x_v[:, 0:FIRST]).then_inc(ld_x0, 16)
            act.dma_start(Wv_raw[:, :], Wv).then_inc(ld_wv, 16)
            def job_hi(i, c, n):
                kind, which = JOB[n]
                act.wait_ge(job_done, JOBS * (2 * i + c) + n + 1)
                par, bank = c % 2, bank_of(2 * i + c if isinstance(i, int) else None, n)
                if kind == "turn":
                    dst, src = tT_hi[:, par, 2 * P * which:2 * P * which + 2 * P], bank[:, 0:2 * P]
                elif kind == "u":
                    dst = u_hi[:, par, 2 * which:2 * which + 2, :]
                    src = bank[:, :].rearrange("p (h t) -> p h t", h=2)
                else:
                    dst = v[:, par, which // 2, 512 * (which % 2):512 * (which % 2) + 512]
                    src = bank[:, :]
                act.activation(dst, src, ACT.Copy).then_inc(job_hi_done, 1)

            def exps(i, c, g):
                act.wait_ge(negmax_done, 16 * i + 2 * c + g + 1)
                if c >= 2:
                    act.wait_ge(turned_done, 16 * i + 2 * (c - 2) + g + 1)
                for h in range(4 * g, 4 * g + 4):
                    e = act.activation(prob[:, c % 2, h, :], masked[:, c % 2, h, :], ACT.Exp,
                                       bias=negmax[:, c % 2, h:h + 1], scale=SCALE,
                                       accum_out=rowsum[:, c % 2, h:h + 1])
                e.then_inc(exp_done, 1)

            def probT_copy(i, c):
                act.wait_ge(turned_done, 16 * i + 2 * c + 1)
                if c >= 2:
                    act.wait_ge(heads_done, 8 * i + c - 1)
                act.activation(probT[:, c % 2, 0:4, :], T0[:, :].rearrange("p (h j) -> p h j", h=4),
                               ACT.Copy).then_inc(probT0_done, 1)

            def slot(i, c):
                jobs = slot_jobs(i, c)
                if exists(i, c - 1):
                    exps(i, c - 1, 1)
                for pair, n in jobs[0:2]:
                    job_hi(i, pair, n)
                if exists(i, c - 1):
                    probT_copy(i, c - 1)
                if exists(i, c):
                    exps(i, c, 0)
                for pair, n in jobs[2:]:
                    job_hi(i, pair, n)

            for n in range(2):
                act.wait_ge(w_turned, n + 1)
                act.activation(WqT[:, 4 * n:4 * n + 4, :],
                               score_bank[n][:, :].rearrange("p (c d) -> p c d", d=P), ACT.Copy)\
                    .then_inc(wqT_ready, 1)
            job_hi(0, 0, 0)
            act.wait_ge(ld_wv, 16)
            act.activation(Wv_hi[:, :], Wv_raw[:, :], ACT.Copy).then_inc(wv_hi_ready, 1)
            for n, bank in enumerate(M_BANKS):
                act.wait_ge(m_ready, n + 1)
                h0 = n % 2 + STEP_HEADS * (n // 2)
                act.activation(M_hi[:, h0:h0 + 7:2, :], bank[:, :].rearrange("p (h d) -> p h d", d=P),
                               ACT.Copy).then_inc(m_hi_ready, 1)
                if n == 1:
                    job_hi(0, 0, 1)
            act.wait_ge(ld_gate, 32)
            act.activation(gates[:, :], gates[:, :], ACT.Tanh).then_inc(gates_ready, 1)
            for n in range(2, JOBS):
                job_hi(0, 0, n)
            job_hi(0, 1, 0)
            job_hi(0, 1, 1)
            for c in range(LEAD):
                slot(0, c)
            with act.Fori(0, STEPS // BODY - 1) as i:
                for c in range(LEAD, LEAD + BODY):
                    slot(i, c)

            def turned_hi(i, c):
                act.wait_ge(f_turned, 2 * i + c + 1)
                act.activation(x2T_hi[:, c % 2], J0[:, :], ACT.Copy).then_inc(f_hi, 1)

            def gelu(i, c, f):
                act.wait_ge(f_up, 4 * (2 * i + c) + f + 1)
                if c >= 2:
                    act.wait_ge(f_down, 2 * i + c - 1)
                act.activation(hid[:, c % 2, f], score_bank[f % 2][:, :], ACT.Gelu,
                               bias=bfc[:, f:f + 1]).then_inc(f_gelu, 1)

            def group(i, c):
                for f in range(CHUNKS):
                    if exists(i, c, GROUPS, 2):
                        gelu(i, c, f)
                    if f == 1 and exists(i, c + 1, GROUPS, 2):
                        turned_hi(i, c + 1)

            for c in range(LEAD, LEAD + BODY):
                slot(STEPS // BODY - 1, c)
                if c == 6:
                    act.wait_ge(wm_turned, 1)
                    act.activation(W1_hi[:, :], J0[:, :], ACT.Copy).then_inc(w1_hi_ready, 1)
                if c == 7:
                    turned_hi(0, 0)
            act.wait_ge(ld_lora, 80)
            for c in range(3):
                group(0, c)
            with act.Fori(0, GROUPS // 2 - 2) as i:
                group(i, 3)
                group(i, 4)
            group(GROUPS // 2 - 2, 3)

        @block.vector
        def _(dve):
            def pair_stats(i, c):
                k = 5 * (2 * i + c)
                for r in range(2):
                    dve.bn_stats(stats[:, 2 * (c % 2) + r, :],
                                 X[:, bass.ds((4 * i + 2 * c + r) * P, P)]).then_inc(ln_stats, 1)
                dve.wait_ge(ln_stats, k + 2)
                dve.sem_inc(passed, 1)
                for r in range(2):
                    s = 2 * (c % 2) + r
                    dve.bn_aggr(meanvar[:, s, :], stats[:, s, :]).then_inc(ln_stats, 1)
                dve.wait_ge(ln_stats, k + 4)
                mv = meanvar[:, 2 * (c % 2):2 * (c % 2) + 2, 1]
                dve.tensor_scalar(mv, mv, EPS, None, ALU.add).then_inc(ln_stats, 1)

            def pair_norm(i, c):
                dve.wait_ge(ln_rstd, 2 * i + c + 1)
                for r in range(2):
                    s = 2 * (c % 2) + r
                    n = dve.tensor_scalar(xn[:, c % 2, P * r:P * r + P],
                                          X[:, bass.ds((4 * i + 2 * c + r) * P, P)],
                                          meanvar[:, s, 0:1], rstd[:, s:s + 1],
                                          ALU.subtract, ALU.mult)
                n.then_inc(ln_done, 1)

            def job_lo(i, c, n):
                kind, which = JOB[n]
                if kind == "v":
                    return
                dve.wait_ge(job_hi_done, JOBS * (2 * i + c) + n + 1)
                par, bank = c % 2, bank_of(2 * i + c if isinstance(i, int) else None, n)
                if kind == "turn":
                    cut = slice(2 * P * which, 2 * P * which + 2 * P)
                    dst, hi, src = tT_lo[:, par, cut], tT_hi[:, par, cut], bank[:, 0:2 * P]
                else:
                    cut = slice(2 * which, 2 * which + 2)
                    dst, hi = u_lo[:, par, cut, :], u_hi[:, par, cut, :]
                    src = bank[:, :].rearrange("p (h t) -> p h t", h=2)
                dve.tensor_tensor(dst, src, hi.bitcast(F32), ALU.subtract).then_inc(job_lo_done, 1)

            def batch_bias(i, c):
                dve.scalar_tensor_tensor(out=bias[:, c // 2 % 2, :],
                                         in0=maskb[:, bass.ds((4 * i + c // 2) * P, P)], scalar=-FMAX,
                                         in1=causal[:, :], op0=ALU.mult, op1=ALU.min)\
                    .then_inc(bias_done, 1)

            def mask_max(i, c, g):
                if g == 0:
                    dve.wait_ge(bias_done, 4 * i + c // 2 + 1)
                dve.wait_ge(scores_done, 16 * i + 2 * c + g + 1)
                if c >= 2:
                    dve.wait_ge(exp_done, 16 * i + 2 * (c - 2) + g + 1)
                dve.sem_inc(passed, 1)
                for n in range(4):
                    h = 4 * g + n
                    m = dve.tensor_tensor_reduce(masked[:, c % 2, h, :],
                                                 score_bank[g][:, n * P:n * P + P],
                                                 bias[:, c // 2 % 2, :], 1.0, -FMAX, ALU.add, ALU.max,
                                                 rowmax[:, c % 2, h:h + 1])
                m.then_inc(masked_done, 1)
                dve.wait_ge(masked_done, 16 * i + 2 * c + g + 1)
                cut = slice(4 * g, 4 * g + 4)
                dve.tensor_scalar(negmax[:, c % 2, cut], rowmax[:, c % 2, cut], -SCALE, None, ALU.mult)\
                    .then_inc(negmax_done, 1)

            def inverse(i, c, g):
                dve.wait_ge(exp_done, 16 * i + 2 * c + g + 1)
                cut = slice(4 * g, 4 * g + 4)
                dve.reciprocal(invsum[:, c % 2, cut], rowsum[:, c % 2, cut]).then_inc(inv_done, 1)

            def probT_copy(i, c):
                dve.wait_ge(turned_done, 16 * i + 2 * c + 2)
                if c >= 2:
                    dve.wait_ge(heads_done, 8 * i + c - 1)
                dve.tensor_copy(probT[:, c % 2, 4:8, :], T1[:, :].rearrange("p (h j) -> p h j", h=4))\
                    .then_inc(probT1_done, 1)

            def headT_copy(i, c):
                dve.wait_ge(heads_done, 8 * i + c + 1)
                dve.tensor_copy(headT[:, c % 2, :], OB[:, :]).then_inc(headT_done, 1)

            def add_y(i, c):
                dve.wait_ge(y_done, 8 * i + c + 1)
                dve.wait_ge(resid_done, 2 * i + c // 4 + 1)
                xb = X[:, bass.ds((4 * i + c // 2) * P, P)]
                dve.tensor_tensor(xb, YB[:, 0:P], xb, ALU.add).then_inc(x_done, 1)

            def slot(i, c):
                jobs = slot_jobs(i, c)
                ln = c % 4 == 3 and exists(i, c // 4 + 2, PAIRS, 2)
                if exists(i, c) and c % 2 == 0:
                    batch_bias(i, c)
                if c >= 1:
                    for pair, n in slot_jobs(i, c - 1)[2:]:
                        job_lo(i, pair, n)
                if exists(i, c):
                    mask_max(i, c, 0)
                if exists(i, c - 1):
                    inverse(i, c - 1, 1)
                if exists(i, c):
                    mask_max(i, c, 1)
                if ln:
                    pair_stats(i, c // 4 + 2)
                for pair, n in jobs[0:1]:
                    job_lo(i, pair, n)
                if exists(i, c - 2):
                    headT_copy(i, c - 2)
                if exists(i, c - 1):
                    probT_copy(i, c - 1)
                for pair, n in jobs[1:2]:
                    job_lo(i, pair, n)
                if exists(i, c - 3) and c % 2 == 0:
                    add_y(i, c - 3)
                if ln:
                    pair_norm(i, c // 4 + 2)
                if exists(i, c):
                    inverse(i, c, 0)

            dve.wait_ge(ld_x0, 16)
            pair_stats(0, 0)
            for n in range(2):
                dve.wait_ge(w_turned, n + 3)
                dve.tensor_copy(WkT[:, 4 * n:4 * n + 4, :],
                                turn_bank[n][:, :].rearrange("p (c d) -> p c d", d=P))\
                    .then_inc(wkT_ready, 1)
            pair_norm(0, 0)
            job_lo(0, 0, 0)
            pair_stats(0, 1)
            for n, bank in enumerate(M_BANKS):
                dve.wait_ge(m_hi_ready, n + 1)
                cut = slice(n % 2 + STEP_HEADS * (n // 2), n % 2 + STEP_HEADS * (n // 2) + 7, 2)
                dve.tensor_tensor(M_lo[:, cut, :], bank[:, :].rearrange("p (h d) -> p h d", d=P),
                                  M_hi[:, cut, :].bitcast(F32), ALU.subtract).then_inc(m_lo_ready, 1)
                if n == 1:
                    job_lo(0, 0, 1)
            pair_norm(0, 1)
            for n in range(2, JOBS):
                job_lo(0, 0, n)
            job_lo(0, 1, 0)
            job_lo(0, 1, 1)
            dve.wait_ge(gates_ready, 1)
            dve.wait_ge(ld_bias, 32)
            for n in range(2):
                dve.tensor_scalar(gbias[:, n, :], gbias[:, n, :], gates[:, n:n + 1], None, ALU.mult)\
                    .then_inc(gbias_ready, 1)
            dve.wait_ge(ld_wo, 16)
            dve.tensor_scalar(Wo_sb[:, :, :], Wo_sb[:, :, :], gates[:, 0:1], None, ALU.mult)\
                .then_inc(wo_ready, 1)
            dve.wait_ge(ld_mask, 16)
            dve.wait_ge(consts_set, 3)
            for c in range(LEAD):
                slot(0, c)
            dve.wait_ge(ld_x1, 16)
            with dve.Fori(0, STEPS // BODY - 1) as i:
                for c in range(LEAD, LEAD + BODY):
                    slot(i, c)

            def weight_max():
                dve.wait_ge(ld_ffn, 32)
                for n in range(2):
                    dve.tensor_reduce(wabs[:, n:n + 1], Wf[:, n, :], AX.X, ALU.max).then_inc(wprep, 1)
                    dve.tensor_reduce(wabs[:, 2 + n:3 + n], Wf[:, n, :], AX.X, ALU.min)\
                        .then_inc(wprep, 1)
                dve.wait_ge(wprep, 4)
                for n in range(2):
                    dve.scalar_tensor_tensor(out=wabs[:, 4 + n:5 + n], in0=wabs[:, 2 + n:3 + n],
                                             scalar=-1.0, in1=wabs[:, n:n + 1], op0=ALU.mult,
                                             op1=ALU.max).then_inc(wprep, 1)

            def lora_b():
                dve.wait_ge(bT_turned, 1)
                dve.tensor_copy(BT[:, 0:FF], J0[0:RANK, :]).then_inc(bT_ready, 1)
                dve.tensor_copy(BT[:, FF:FF + P], J1[0:RANK, 0:P]).then_inc(bT_ready, 1)

            def weight_quant():
                dve.wait_ge(wmax_ready, 1)
                dve.tensor_scalar(wscale[:, 0:2], wall[:, :], 1.0 / QMAX, None, ALU.mult)\
                    .then_inc(wprep, 1)
                dve.wait_ge(wprep, 7)
                dve.reciprocal(wscale[:, 2:4], wscale[:, 0:2]).then_inc(wprep, 1)
                for n in range(2):
                    dve.wait_ge(wprep, 8 + 3 * n)
                    dve.tensor_scalar(Wt[:, n, :], Wf[:, n, :], wscale[:, 2 + n:3 + n], ROUND,
                                      ALU.mult, ALU.add).then_inc(wprep, 1)
                    dve.wait_ge(wprep, 9 + 3 * n)
                    dve.tensor_scalar(Wt[:, n, :], Wt[:, n, :], ROUND, QMAX, ALU.subtract, ALU.min)\
                        .then_inc(wprep, 1)
                    dve.wait_ge(wprep, 10 + 3 * n)
                    dve.tensor_scalar(Wt[:, n, :], Wt[:, n, :], -QMAX - 1, wscale[:, n:n + 1],
                                      ALU.max, ALU.mult).then_inc(wprep, 1)
                dve.wait_ge(lora_ready, 1)
                dve.wait_ge(wprep, 14)
                for n in range(2):
                    dve.scalar_tensor_tensor(out=Wt[:, n, :], in0=job_bank[n][:, :],
                                             scalar=LORA_SCALE, in1=Wt[:, n, :], op0=ALU.mult,
                                             op1=ALU.add).then_inc(wprep, 1)

            def weight_split():
                dve.wait_ge(w1_hi_ready, 1)
                dve.tensor_tensor(W1_lo[:, :], J0[:, :], W1_hi[:, :].bitcast(F32), ALU.subtract)\
                    .then_inc(w12_ready, 1)
                dve.tensor_scalar(W2T[:, :, :], J1[:, :].rearrange("p (c d) -> p c d", d=P),
                                  gates[:, 1:2], None, ALU.mult).then_inc(w12_ready, 1)

            def group_stats(i, c):
                k = 5 * (2 * i + c)
                for b in range(4):
                    s = dve.bn_stats(stats[:, b, :], X[:, bass.ds((8 * i + 4 * c + b) * P, P)])
                    s.then_inc(f_stats, 1) if b in (1, 3) else None
                dve.wait_ge(f_stats, k + 2)
                dve.sem_inc(passed, 1)
                for b in range(4):
                    s = dve.bn_aggr(meanvar[:, b, :], stats[:, b, :])
                    s.then_inc(f_stats, 1) if b in (1, 3) else None
                dve.wait_ge(f_stats, k + 4)
                dve.tensor_scalar(meanvar[:, :, 1], meanvar[:, :, 1], EPS, None, ALU.add)\
                    .then_inc(f_stats, 1)

            def group_norm(i, c):
                dve.wait_ge(f_rstd, 2 * i + c + 1)
                if c >= 2:
                    dve.wait_ge(f_turned, 2 * i + c - 1)
                for b in range(4):
                    n = dve.tensor_scalar(xn2[c % 2][:, b * P:b * P + P],
                                          X[:, bass.ds((8 * i + 4 * c + b) * P, P)],
                                          meanvar[:, b, 0:1], rstd[:, b:b + 1],
                                          ALU.subtract, ALU.mult)
                n.then_inc(f_norm, 1)

            def turned_lo(i, c):
                dve.wait_ge(f_hi, 2 * i + c + 1)
                dve.tensor_tensor(x2T_lo[:, c % 2], J0[:, :], x2T_hi[:, c % 2].bitcast(F32),
                                  ALU.subtract).then_inc(f_lo, 1)

            def group_out(i, c):
                dve.wait_ge(f_down, 2 * i + c + 1)
                dve.wait_ge(f_resid, 2 * i + c + 1)
                xg = X[:, bass.ds((8 * i + 4 * c) * P, 4 * P)]
                dve.tensor_tensor(xg, turn_bank[c % 2][:, :], xg, ALU.add).then_inc(f_out, 1)

            def group(i, c):
                if exists(i, c + 1, GROUPS, 2):
                    group_stats(i, c + 1)
                    group_norm(i, c + 1)
                if exists(i, c + 1, GROUPS, 2):
                    turned_lo(i, c + 1)
                if exists(i, c - 1, GROUPS, 2):
                    group_out(i, c - 1)

            for c in range(LEAD, LEAD + BODY):
                slot(STEPS // BODY - 1, c)
                if c == 4:
                    weight_max()
                    lora_b()
                if c == 5:
                    weight_quant()
                if c == 6:
                    weight_split()
                    dve.wait_ge(x_done, 4)
                    group_stats(0, 0)
                if c == 7:
                    group_norm(0, 0)
                if c == 8:
                    turned_lo(0, 0)
            dve.wait_ge(x_done, BATCHES)
            for c in range(3):
                group(0, c)
            with dve.Fori(0, GROUPS // 2 - 2) as i:
                group(i, 3)
                group(i, 4)
            group(GROUPS // 2 - 2, 3)
            group(GROUPS // 2 - 2, 4)

        @block.tensor
        def _(pe):
            def split3(dst, w_hi, w_lo, m_hi, m_lo):
                pe.matmul(dst, w_hi, m_hi, start=True, stop=False)
                pe.matmul(dst, w_hi, m_lo, start=False, stop=False)
                return pe.matmul(dst, w_lo, m_hi, start=False, stop=True)

            pe.wait_ge(ident_set, 2)
            for w, loaded, banks in ((Wq_sb, ld_wq, score_bank), (Wk_sb, ld_wk, turn_bank)):
                pe.wait_ge(loaded, 16)
                for n in range(2):
                    for c in range(4):
                        t = pe.transpose(banks[n][:, c * P:c * P + P],
                                         w[:, (4 * n + c) * P:(4 * n + c + 1) * P], ident[:, :])
                    t.then_inc(w_turned, 1)

            def job(i, c, n):
                kind, which = JOB[n]
                par, bank = c % 2, bank_of(2 * i + c if isinstance(i, int) else None, n)
                pair = 2 * i + c
                first = isinstance(i, int) and pair == 0
                if n == 2 and first:
                    pe.wait_ge(m_lo_ready, 2)
                if n == 4 and first:
                    pe.wait_ge(m_lo_ready, 4)
                    pe.wait_ge(wv_lo_ready, 1)
                if first and n >= 6:
                    pe.wait_ge(job_hi_done, n - 5)
                    pe.wait_ge(job_lo_done, splits_before(n - 5))
                if not first:
                    last = JOBS * pair + n - 2
                    pe.wait_ge(job_hi_done, last + 1)
                    if JOB[n - 2][0] != "v":
                        pe.wait_ge(job_lo_done, NSPLIT * pair + (
                            splits_before(n - 1) if n >= 2 else splits_before(JOBS + n - 1) - NSPLIT))
                if kind == "turn":
                    if which == 0:
                        pe.wait_ge(ln_done, pair + 1)
                    else:
                        pe.wait_ge((ld_c0, ld_c1)[par], 16 * (i + c // 2 + 1))
                    for r in range(2):
                        m = pe.transpose(bank[:, r * P:r * P + P],
                                         (xn, C)[which][:, par, r * P:r * P + P], ident[:, :])
                elif kind == "u":
                    pe.wait_ge(job_lo_done, NSPLIT * pair + splits_before(1))
                    for r in range(2):
                        h = 2 * which + r
                        m = split3(bank[:, 256 * r:256 * r + 256], M_hi[:, h, :], M_lo[:, h, :],
                                   tT_hi[:, par, 2 * P:4 * P], tT_lo[:, par, 2 * P:4 * P])
                else:
                    cols = slice(512 * (which % 2), 512 * (which % 2) + 512)
                    keys = slice((2 + which // 2) * P, (3 + which // 2) * P)
                    m = split3(bank[:, :], tT_hi[:, par, keys], tT_lo[:, par, keys],
                               Wv_hi[:, cols], Wv_lo[:, cols])
                m.then_inc(job_done, 1)

            def scores(i, c):
                r, half = c // 2 % 2, c % 2
                par = c // 4 % 2
                pair = 2 * i + c // 4
                pe.wait_ge(job_lo_done,
                           NSPLIT * pair + splits_before(JOB.index(("u", 4 * half + 3)) + 1))
                if isinstance(i, int) and 8 * i + c == 0:
                    pe.wait_ge(job_hi_done, JOBS - 2)
                    pe.wait_ge(job_lo_done, splits_before(JOBS - 2))
                for g in range(2):
                    if c >= 1:
                        pe.wait_ge(masked_done, 16 * i + 2 * (c - 1) + g + 1)
                    hs = slice(8 * half + 4 * g, 8 * half + 4 * g + 4)
                    split3(score_bank[g][:, :].rearrange("p (h j) -> p h j", h=4),
                           tT_hi[:, par, r * P:r * P + P], tT_lo[:, par, r * P:r * P + P],
                           u_hi[:, par, hs, r * P:r * P + P], u_lo[:, par, hs, r * P:r * P + P])\
                        .then_inc(scores_done, 1)

            def turn(i, c):
                for g in range(2):
                    pe.wait_ge(prob_done, 16 * i + 2 * c + g + 1)
                    if c >= 1:
                        pe.wait_ge((probT0_done, probT1_done)[g], 8 * i + c)
                    for n in range(4):
                        t = pe.transpose(turn_bank[g][:, n * P:n * P + P],
                                         prob[:, c % 2, 4 * g + n, :], ident[:, :])
                    t.then_inc(turned_done, 1)

            def attend(i, c):
                par, r, half = c // 4 % 2, c // 2 % 2, c % 2
                pe.wait_ge(job_hi_done, JOBS * (2 * i + c // 4) + JOB.index(("v", 2 * r + 1)) + 1)
                if c >= 1:
                    pe.wait_ge(headT_done, 8 * i + c)
                pe.wait_ge(probT0_done, 8 * i + c + 1)
                for h in range(STEP_HEADS):
                    if h == 4:
                        pe.wait_ge(probT1_done, 8 * i + c + 1)
                    rows = slice(DH * (h % 2), DH * (h % 2) + DH)
                    col = (8 * half + h) * DH
                    m = pe.matmul(OB[rows, h // 2 * P:h // 2 * P + P], v[:, par, r, col:col + DH],
                                  probT[:, c % 2, h, :], start=True, stop=True)
                m.then_inc(heads_done, 1)

            def project(i, c):
                half = c % 2
                if half == 0 and c >= 2:
                    pe.wait_ge(x_done, 4 * i + c // 2)
                pe.wait_ge(headT_done, 8 * i + c + 1)
                if isinstance(i, int) and 8 * i + c == 0:
                    pe.wait_ge(wo_ready, 1)
                for q in range(4):
                    m = pe.matmul(YB[:, 0:P], headT[:, c % 2, q * P:q * P + P],
                                  Wo_sb[:, 4 * half + q, :], start=(half == 0 and q == 0),
                                  stop=(half == 1 and q == 3))
                m.then_inc(y_done, 1)

            def slot(i, c):
                jobs = slot_jobs(i, c)
                if exists(i, c):
                    scores(i, c)
                for pair, n in jobs[0:2]:
                    job(i, pair, n)
                if exists(i, c - 1):
                    turn(i, c - 1)
                for pair, n in jobs[2:3]:
                    job(i, pair, n)
                if exists(i, c - 1):
                    attend(i, c - 1)
                for pair, n in jobs[3:]:
                    job(i, pair, n)
                if exists(i, c - 2):
                    project(i, c - 2)

            job(0, 0, 0)
            pe.wait_ge(wqT_ready, 2)
            pe.wait_ge(wkT_ready, 2)
            for n, bank in enumerate(M_BANKS):
                rows = slice(DH * (n % 2), DH * (n % 2) + DH)
                for k in range(4):
                    ch = 4 * (n // 2) + k
                    m = pe.matmul(bank[:, k * P:k * P + P], WkT[rows, ch, :], WqT[rows, ch, :],
                                  start=True, stop=True)
                m.then_inc(m_ready, 1)
                if n == 1:
                    job(0, 0, 1)
            for n in range(2, JOBS):
                job(0, 0, n)
            job(0, 1, 0)
            job(0, 1, 1)
            for c in range(LEAD):
                slot(0, c)
            with pe.Fori(0, STEPS // BODY - 1) as i:
                for c in range(LEAD, LEAD + BODY):
                    slot(i, c)
            def lora_b():
                pe.wait_ge(ld_lora, 80)
                pe.wait_ge(job_hi_done, JOBS * PAIRS)
                pe.wait_ge(job_lo_done, NSPLIT * PAIRS)
                for c in range(CHUNKS):
                    pe.transpose(J0[0:RANK, c * P:c * P + P], Bfc[:, c, :], ident[:, :])
                pe.transpose(J1[0:RANK, 0:P], Bpr[:, :], ident[:, :]).then_inc(bT_turned, 1)

            def lora_ba():
                pe.wait_ge(bT_ready, 2)
                for c in range(CHUNKS):
                    pe.matmul(J0[:, c * P:c * P + P], BT[:, c * P:c * P + P], Afc[:, :],
                              start=True, stop=True)
                pe.matmul(J1[:, :], BT[:, FF:FF + P], Apr[:, :], start=True, stop=True)\
                    .then_inc(lora_ready, 1)

            def turn_weights():
                pe.wait_ge(wprep, 16)
                for n in range(2):
                    for c in range(CHUNKS):
                        t = pe.transpose(job_bank[n][:, c * P:c * P + P], Wt[:, n, c * P:c * P + P],
                                         ident[:, :])
                t.then_inc(wm_turned, 1)

            def turn_x(i, c):
                pe.wait_ge(f_norm, 2 * i + c + 1)
                if c >= 1:
                    pe.wait_ge(f_lo, 2 * i + c)
                for b in range(4):
                    t = pe.transpose(J0[:, b * P:b * P + P], xn2[c % 2][:, b * P:b * P + P],
                                     ident[:, :])
                t.then_inc(f_turned, 1)

            def up(i, c, f):
                pe.wait_ge(f_lo, 2 * i + c + 1)
                if c >= 1 or f >= 2:
                    pe.wait_ge(f_gelu, 4 * (2 * i + c) + f - 1)
                split3(score_bank[f % 2][:, :], W1_hi[:, f * P:f * P + P], W1_lo[:, f * P:f * P + P],
                       x2T_hi[:, c % 2], x2T_lo[:, c % 2]).then_inc(f_up, 1)

            def down(i, c, t):
                pe.wait_ge(f_gelu, 4 * (2 * i + c) + 4)
                if c >= 2:
                    pe.wait_ge(f_out, 2 * i + c - 1)
                for f in range(CHUNKS):
                    m = pe.matmul(turn_bank[c % 2][:, t * P:t * P + P],
                                  hid[:, c % 2, f, t * P:t * P + P], W2T[:, f, :],
                                  start=(f == 0), stop=(f == CHUNKS - 1))
                if t == 3:
                    m.then_inc(f_down, 1)

            def group(i, c):
                for f in range(CHUNKS):
                    if exists(i, c, GROUPS, 2):
                        up(i, c, f)
                    if exists(i, c - 1, GROUPS, 2):
                        down(i, c - 1, f)
                    if f == 1 and exists(i, c + 1, GROUPS, 2):
                        turn_x(i, c + 1)

            for c in range(LEAD, LEAD + BODY):
                slot(STEPS // BODY - 1, c)
                if c == 4:
                    lora_b()
                if c == 5:
                    lora_ba()
                if c == 6:
                    turn_weights()
                if c == 7:
                    pe.wait_ge(w12_ready, 2)
                    turn_x(0, 0)
            for c in range(3):
                group(0, c)
            with pe.Fori(0, GROUPS // 2 - 2) as i:
                group(i, 3)
                group(i, 4)
            group(GROUPS // 2 - 2, 3)
            group(GROUPS // 2 - 2, 4)


_INS = ["x", "ctx_1024", "mask_BxS2_bf0", "g_xattn", "g_ffn", "L0_xattn_Wq", "L0_xattn_Wk",
        "L0_xattn_Wv", "L0_xattn_Wo", "L0_xattn_bo", "L0_ffn_W_fc", "L0_ffn_b_fc", "L0_ffn_A_fc",
        "L0_ffn_B_fc", "L0_ffn_W_proj", "L0_ffn_b_proj", "L0_ffn_A_proj", "L0_ffn_B_proj"]


def kernel(**inputs):
    import concourse.bacc as bacc
    from concourse.bass_utils import run_bass_kernel_spmd

    nc = bacc.Bacc("TRN2", target_bir_lowering=False, num_devices=1)
    arrays, args = {}, []
    for name in _INS:
        a = np.ascontiguousarray(inputs[name])
        arrays[f"in_{name}"] = a
        args.append(nc.dram_tensor(f"in_{name}", a.shape, mybir.dt.from_np(a.dtype),
                                   kind="ExternalInput").ap())
    args.append(nc.dram_tensor("out", (BATCHES, P, P), F32, kind="ExternalOutput").ap())
    build(nc, *args)
    r = run_bass_kernel_spmd(nc, [arrays], core_ids=[0])
    return r.results[0]["out"]
```

```python
from contextlib import ExitStack

import concourse.bass as bass
import concourse.mybir as mybir
import numpy as np

F32 = mybir.dt.float32
F32R = mybir.dt.float32r
ALU = mybir.AluOpType
ACT = mybir.ActivationFunctionType
AX = mybir.AxisListType
RMAX = bass.bass_isa.ReduceOp.max

P = 128
BATCHES, HEADS, DH = 32, 16, 64
INNER = HEADS * DH
FF, RANK = 512, 16
CHUNKS = FF // P
SCALE = DH ** -0.5
EPS = 1e-5
FMAX = float(np.finfo(np.float32).max)
QMAX = 127.0
LORA_SCALE = 2.0
ROUND = 12582912.0

PAIRS = BATCHES // 2
STEP_HEADS = 8
STEPS = BATCHES * HEADS // STEP_HEADS
BODY = 8
LEAD = 3
JOBS = 14
JOB = [("turn", 1), ("u", 0), ("u", 1), ("v", 0), ("u", 2), ("u", 3), ("v", 1),
       ("u", 4), ("u", 5), ("v", 2), ("turn", 0), ("u", 6), ("u", 7), ("v", 3)]
SPLITS = [n for n, (kind, _) in enumerate(JOB) if kind != "v"]
NSPLIT = len(SPLITS)
GROUPS = BATCHES // 4


def splits_before(n):
    return sum(m < n for m in SPLITS)


def slot_jobs(i, c):
    k, jobs = c % 4, []
    if exists(i, c // 4 + 1, PAIRS, 2):
        jobs += [(c // 4 + 1, n) for n in ((1, 2, 3), (4, 5, 6), (7, 8, 9, 10), (11, 12, 13))[k]]
    if k == 3 and exists(i, c // 4 + 2, PAIRS, 2):
        jobs += [(c // 4 + 2, 0)]
    return jobs


def exists(i, c, end=STEPS, per=BODY):
    return not isinstance(i, int) or 0 <= per * i + c < end


def build(nc, x, ctx, mask, g_xattn, g_ffn, Wq, Wk, Wv, Wo, bo, W_fc, b_fc, A_fc, B_fc, W_proj,
          b_proj, A_proj, B_proj, out):
    st = ExitStack()
    with st:
        def sb(name, shape, dt=F32):
            return st.enter_context(nc.sbuf_tensor(name, shape, dt))

        def sem(name):
            return st.enter_context(nc.semaphore(name))

        X = sb("X", [P, BATCHES * P])
        C = sb("C", [P, 2, 2 * P])
        maskb = sb("maskb", [P, BATCHES * P], mybir.dt.uint8)
        ident = sb("ident", [P, P])
        causal = sb("causal", [P, P])
        bias = sb("bias", [P, 2, P])
        xn = sb("xn", [P, 2, 2 * P])
        tT_hi = sb("tT_hi", [P, 2, 4 * P], F32R)
        tT_lo = sb("tT_lo", [P, 2, 4 * P], F32R)
        u_hi = sb("u_hi", [P, 2, HEADS, 2 * P], F32R)
        u_lo = sb("u_lo", [P, 2, HEADS, 2 * P], F32R)
        v = sb("v", [P, 2, 2, INNER])
        masked = sb("masked", [P, 2, STEP_HEADS, P])
        prob = sb("prob", [P, 2, STEP_HEADS, P])
        probT = sb("probT", [P, 2, STEP_HEADS, P])
        headT = sb("headT", [P, 2, 4 * P])
        rowmax = sb("rowmax", [P, 2, STEP_HEADS])
        negmax = sb("negmax", [P, 2, STEP_HEADS])
        rowsum = sb("rowsum", [P, 2, STEP_HEADS])
        invsum = sb("invsum", [P, 2, STEP_HEADS])
        stats = sb("stats", [P, 4, 6])
        meanvar = sb("meanvar", [P, 4, 2])
        rstd = sb("rstd", [P, 4])
        power = sb("power", [P, 4])
        M_hi = sb("M_hi", [P, HEADS, P], F32R)
        M_lo = sb("M_lo", [P, HEADS, P], F32R)
        Wv_raw = sb("Wv_raw", [P, INNER])
        Wv_hi = sb("Wv_hi", [P, INNER], F32R)
        Wv_lo = sb("Wv_lo", [P, INNER], F32R)
        Wo_sb = sb("Wo_sb", [P, INNER // P, P])
        gates = sb("gates", [P, 2])
        gbias = sb("gbias", [P, 2, P])
        Wf = sb("Wf", [P, 2, FF])
        Wt = sb("Wt", [P, 2, FF])
        W1_hi = sb("W1_hi", [P, FF], F32R)
        W1_lo = sb("W1_lo", [P, FF], F32R)
        W2T = sb("W2T", [P, CHUNKS, P])
        bfc = sb("bfc", [P, CHUNKS])
        Afc = sb("Afc", [RANK, P])
        Apr = sb("Apr", [RANK, FF])
        Bfc = sb("Bfc", [P, CHUNKS, RANK])
        Bpr = sb("Bpr", [P, RANK])
        BT = sb("BT", [RANK, FF + P])
        wabs = sb("wabs", [P, 2])
        wall = sb("wall", [P, 2])
        wscale = sb("wscale", [P, 4])
        Wq_sb, Wk_sb = (probT[:, n].rearrange("p h j -> p (h j)") for n in range(2))
        WqT, WkT = (prob[:, n] for n in range(2))
        hid = v[:, :].rearrange("p a b (f t) -> p a (b f) t", f=2)
        xn2 = (xn[:, :].rearrange("p a t -> p (a t)"), C[:, :].rearrange("p a t -> p (a t)"))
        x2T_hi = u_hi[:, 0, 0:4].rearrange("p (a b) t -> p a (b t)", a=2)
        x2T_lo = u_lo[:, 0, 0:4].rearrange("p (a b) t -> p a (b t)", a=2)

        S0, S1, T0, T1, J0, J1, OB, YB = (
            st.enter_context(nc.psum_tensor(n, [P, 512], F32))
            for n in ("S0", "S1", "T0", "T1", "J0", "J1", "OB", "YB"))
        score_bank, turn_bank, job_bank = (S0, S1), (T0, T1), (J0, J1)
        first_job_bank = (J0, J1, T0, T1, S0, S1)

        def bank_of(pair, n):
            return first_job_bank[n % 6] if pair == 0 else job_bank[n % 2]

        M_BANKS = (OB, YB, S0, S1)

        (ld_wq, ld_wk, ld_x0, ld_c0, ld_x1, ld_c1, ld_mask, ld_wv, ld_wo, ld_bias, ld_gate, ld_ffn,
         ld_lora) = (sem(n) for n in (
             "ld_wq", "ld_wk", "ld_x0", "ld_c0", "ld_x1", "ld_c1", "ld_mask", "ld_wv", "ld_wo",
             "ld_bias", "ld_gate", "ld_ffn", "ld_lora"))
        (ident_set, consts_set, w_turned, wqT_ready, wkT_ready, m_ready, m_hi_ready, m_lo_ready,
         wv_hi_ready, wv_lo_ready, gates_ready, wo_ready, gbias_ready, bT_turned, bT_ready,
         lora_ready, wprep, wmax_ready, wm_turned, w1_hi_ready, w12_ready) = (sem(n) for n in (
             "ident_set", "consts_set", "w_turned", "wqT_ready", "wkT_ready", "m_ready",
             "m_hi_ready", "m_lo_ready", "wv_hi_ready", "wv_lo_ready", "gates_ready", "wo_ready",
             "gbias_ready", "bT_turned", "bT_ready", "lora_ready", "wprep", "wmax_ready",
             "wm_turned", "w1_hi_ready", "w12_ready"))
        (scores_done, masked_done, negmax_done, exp_done, inv_done, prob_done, turned_done,
         probT0_done, probT1_done, heads_done, headT_done, y_done, x_done, bias_done, job_done,
         job_hi_done, job_lo_done, ln_stats, ln_rstd, ln_done, resid_done) = (sem(n) for n in (
             "scores_done", "masked_done", "negmax_done", "exp_done", "inv_done", "prob_done",
             "turned_done", "probT0_done", "probT1_done", "heads_done", "headT_done", "y_done",
             "x_done", "bias_done", "job_done", "job_hi_done", "job_lo_done", "ln_stats", "ln_rstd",
             "ln_done", "resid_done"))
        (f_stats, f_rstd, f_norm, f_turned, f_hi, f_lo, f_up, f_gelu, f_down, f_out, f_resid,
         stored) = (sem(n) for n in (
             "f_stats", "f_rstd", "f_norm", "f_turned", "f_hi", "f_lo", "f_up", "f_gelu", "f_down",
             "f_out", "f_resid", "stored"))
        passed = sem("passed")

        block = st.enter_context(nc.Block())

        x_v = x.rearrange("b p d -> p b d")
        c_v = ctx.rearrange("b p d -> p b d")
        out_v = out.rearrange("b p d -> p b d")
        X_b = X[:, :].rearrange("p (b d) -> p b d", d=P)
        FIRST = 4

        @block.sync
        def _(sp):
            sp.dma_start(Wk_sb, Wk).then_inc(ld_wk, 16)

            def load_ctx(i, c):
                if c >= 2:
                    sp.wait_ge(job_done, JOBS * (2 * i + c - 2) + 1)
                sp.dma_start(C[:, c % 2, :].rearrange("p (b d) -> p b d", d=P),
                             c_v[:, bass.ds(4 * i + 2 * c, 2), :]).then_inc((ld_c0, ld_c1)[c % 2], 16)

            load_ctx(0, 0)
            sp.dma_start(gates[:, 0:1], g_xattn.rearrange("(a b) -> a b", a=1)
                         .to_broadcast([P, 1])).then_inc(ld_gate, 16)
            sp.dma_start(gates[:, 1:2], g_ffn.rearrange("(a b) -> a b", a=1)
                         .to_broadcast([P, 1])).then_inc(ld_gate, 16)
            sp.dma_start(gbias[:, 0, :], bo.rearrange("(a b) -> a b", a=1)
                         .to_broadcast([P, P])).then_inc(ld_bias, 16)
            sp.dma_start(gbias[:, 1, :], b_proj.rearrange("(a b) -> a b", a=1)
                         .to_broadcast([P, P])).then_inc(ld_bias, 16)
            sp.dma_start(Wf[:, 0, :].rearrange("p (c d) -> p c d", d=P),
                         W_fc.rearrange("(c p) d -> p c d", p=P)).then_inc(ld_ffn, 16)
            sp.dma_start(Wf[:, 1, :], W_proj).then_inc(ld_ffn, 16)
            load_ctx(0, 1)
            sp.dma_start(maskb[:, :], mask.rearrange("(a b) j -> a (b j)", a=1)
                         .to_broadcast([P, BATCHES * P])).then_inc(ld_mask, 16)
            sp.dma_start(Wo_sb[:, :, :], Wo.rearrange("(q p) d -> p q d", p=P)).then_inc(ld_wo, 16)
            sp.dma_start(X_b[:, FIRST:BATCHES], x_v[:, FIRST:BATCHES]).then_inc(ld_x1, 16)
            sp.dma_start(Afc[:, :], A_fc).then_inc(ld_lora, 16)
            sp.dma_start(Apr[:, :], A_proj).then_inc(ld_lora, 16)
            sp.dma_start(Bfc[:, :, :], B_fc.rearrange("(c p) r -> p c r", p=P)).then_inc(ld_lora, 16)
            sp.dma_start(Bpr[:, :], B_proj).then_inc(ld_lora, 16)
            with nc.allow_non_contiguous_dma(reason="512 biases, once"):
                sp.dma_start(bfc[:, :], b_fc.rearrange("(c p) -> p c", p=P)).then_inc(ld_lora, 16)

            with sp.Fori(0, PAIRS // 2 - 1) as i:
                load_ctx(i, 2)
                load_ctx(i, 3)

            with sp.Fori(0, GROUPS) as i:
                sp.wait_ge(f_out, i + 1)
                sp.dma_start(out_v[:, bass.ds(4 * i, 4), :],
                             X_b[:, bass.ds(4 * i, 4), :]).then_inc(stored, 16)
            sp.wait_ge(stored, 16 * GROUPS)

        @block.gpsimd
        def _(pool):
            pool.memset(ident[:, :], 0.0).then_inc(ident_set, 1)
            pool.memset(causal[:, :], 0.0).then_inc(consts_set, 1)
            pool.memset(power[:, :], -0.5).then_inc(consts_set, 1)
            pool.wait_ge(ident_set, 1)
            pool.affine_select(out=ident[:, :], in_=ident[:, :], compare_op=ALU.not_equal, fill=1.0,
                               base=0, pattern=[[-1, P]], channel_multiplier=1).then_inc(ident_set, 1)
            pool.wait_ge(consts_set, 1)
            pool.affine_select(out=causal[:, :], in_=causal[:, :], compare_op=ALU.is_ge, fill=-FMAX,
                               base=0, pattern=[[-1, P]], channel_multiplier=1).then_inc(consts_set, 1)
            pool.wait_ge(consts_set, 2)

            def pair_rstd(i, c):
                pool.wait_ge(ln_stats, 5 * (2 * i + c) + 5)
                mv = meanvar[:, 2 * (c % 2):2 * (c % 2) + 2, 1]
                pool.tensor_tensor(rstd[:, 2 * (c % 2):2 * (c % 2) + 2], mv, power[:, 0:2], ALU.pow)\
                    .then_inc(ln_rstd, 1)

            pair_rstd(0, 0)
            def pair_resid(i, c):
                pool.wait_ge(ln_done, 2 * i + c + 1)
                xp = X_b[:, bass.ds(4 * i + 2 * c, 2), :]
                pool.tensor_tensor(xp, xp, gbias[:, 0:1, :].to_broadcast([P, 2, P]), ALU.add)\
                    .then_inc(resid_done, 1)

            def normalise(i, c, g):
                pool.wait_ge(inv_done, 16 * i + 2 * c + g + 1)
                pr = prob[:, c % 2, 4 * g:4 * g + 4, :]
                pool.tensor_tensor(pr, pr, invsum[:, c % 2, 4 * g:4 * g + 4].unsqueeze(2)
                                   .to_broadcast([P, 4, P]), ALU.mult).then_inc(prob_done, 1)

            def slot(i, c):
                if exists(i, c - 1):
                    normalise(i, c - 1, 1)
                if c % 4 == 2 and exists(i, c // 4 + 1, PAIRS, 2):
                    pair_rstd(i, c // 4 + 1)
                if exists(i, c):
                    normalise(i, c, 0)
                if c % 4 == 2 and exists(i, c // 4 + 1, PAIRS, 2):
                    pair_resid(i, c // 4 + 1)

            pool.wait_ge(wv_hi_ready, 1)
            pool.tensor_tensor(Wv_lo[:, :], Wv_raw[:, :], Wv_hi[:, :].bitcast(F32), ALU.subtract)\
                .then_inc(wv_lo_ready, 1)
            pool.wait_ge(wprep, 2)
            pool.partition_all_reduce(wall[:, :], wabs[:, :], P, RMAX).then_inc(wmax_ready, 1)
            pool.wait_ge(gbias_ready, 2)
            pair_resid(0, 0)
            for c in range(LEAD):
                slot(0, c)
            with pool.Fori(0, STEPS // BODY - 1) as i:
                for c in range(LEAD, LEAD + BODY):
                    slot(i, c)

            def group_rstd(i, c):
                pool.wait_ge(f_stats, 5 * (2 * i + c) + 5)
                pool.tensor_tensor(rstd[:, :], meanvar[:, :, 1], power[:, :], ALU.pow)\
                    .then_inc(f_rstd, 1)

            def group_resid(i, c):
                pool.wait_ge(f_norm, 2 * i + c + 1)
                xg = X_b[:, bass.ds(8 * i + 4 * c, 4), :]
                pool.tensor_tensor(xg, xg, gbias[:, 1:2, :].to_broadcast([P, 4, P]), ALU.add)\
                    .then_inc(f_resid, 1)

            for c in range(LEAD, BODY + 1):
                slot(STEPS // BODY - 1, c)
                if c == 5:
                    group_rstd(0, 0)
                if c == 7:
                    group_rstd(0, 1)
                if c == 8:
                    group_resid(0, 0)
            group_resid(0, 1)
            with pool.Fori(1, GROUPS // 2) as i:
                for c in range(2):
                    group_rstd(i, c)
                    group_resid(i, c)

        @block.scalar
        def _(act):
            act.dma_start(Wq_sb, Wq).then_inc(ld_wq, 16)
            act.dma_start(X_b[:, 0:FIRST], x_v[:, 0:FIRST]).then_inc(ld_x0, 16)
            act.dma_start(Wv_raw[:, :], Wv).then_inc(ld_wv, 16)
            def job_hi(i, c, n):
                kind, which = JOB[n]
                act.wait_ge(job_done, JOBS * (2 * i + c) + n + 1)
                par, bank = c % 2, bank_of(2 * i + c if isinstance(i, int) else None, n)
                if kind == "turn":
                    dst, src = tT_hi[:, par, 2 * P * which:2 * P * which + 2 * P], bank[:, 0:2 * P]
                elif kind == "u":
                    dst = u_hi[:, par, 2 * which:2 * which + 2, :]
                    src = bank[:, :].rearrange("p (h t) -> p h t", h=2)
                else:
                    dst = v[:, par, which // 2, 512 * (which % 2):512 * (which % 2) + 512]
                    src = bank[:, :]
                act.activation(dst, src, ACT.Copy).then_inc(job_hi_done, 1)

            def exps(i, c, g):
                act.wait_ge(negmax_done, 8 * i + c + 1)
                if c >= 2:
                    act.wait_ge(turned_done, 16 * i + 2 * (c - 2) + g + 1)
                for h in range(4 * g, 4 * g + 4):
                    e = act.activation(prob[:, c % 2, h, :], masked[:, c % 2, h, :], ACT.Exp,
                                       bias=negmax[:, c % 2, h:h + 1], scale=SCALE,
                                       accum_out=rowsum[:, c % 2, h:h + 1])
                e.then_inc(exp_done, 1)

            def probT_copy(i, c):
                act.wait_ge(turned_done, 16 * i + 2 * c + 1)
                if c >= 2:
                    act.wait_ge(heads_done, 8 * i + c - 1)
                act.activation(probT[:, c % 2, 0:4, :], T0[:, :].rearrange("p (h j) -> p h j", h=4),
                               ACT.Copy).then_inc(probT0_done, 1)

            def slot(i, c):
                jobs = slot_jobs(i, c)
                if exists(i, c - 1):
                    exps(i, c - 1, 1)
                if c % 4 == 3:
                    for pair, n in slot_jobs(i, c - 1)[3:]:
                        job_hi(i, pair, n)
                for pair, n in jobs[0:2]:
                    job_hi(i, pair, n)
                if exists(i, c - 1):
                    probT_copy(i, c - 1)
                if exists(i, c):
                    exps(i, c, 0)
                for pair, n in jobs[2:3] if c % 4 == 2 else jobs[2:]:
                    job_hi(i, pair, n)

            for n in range(2):
                act.wait_ge(w_turned, n + 1)
                act.activation(WqT[:, 4 * n:4 * n + 4, :],
                               score_bank[n][:, :].rearrange("p (c d) -> p c d", d=P), ACT.Copy)\
                    .then_inc(wqT_ready, 1)
            job_hi(0, 0, 0)
            act.wait_ge(ld_wv, 16)
            act.activation(Wv_hi[:, :], Wv_raw[:, :], ACT.Copy).then_inc(wv_hi_ready, 1)
            for n, bank in enumerate(M_BANKS):
                act.wait_ge(m_ready, n + 1)
                h0 = n % 2 + STEP_HEADS * (n // 2)
                act.activation(M_hi[:, h0:h0 + 7:2, :], bank[:, :].rearrange("p (h d) -> p h d", d=P),
                               ACT.Copy).then_inc(m_hi_ready, 1)
            act.wait_ge(ld_gate, 32)
            act.activation(gates[:, :], gates[:, :], ACT.Tanh).then_inc(gates_ready, 1)
            for n in range(1, JOBS):
                job_hi(0, 0, n)
            job_hi(0, 1, 0)
            for c in range(LEAD):
                slot(0, c)
            with act.Fori(0, STEPS // BODY - 1) as i:
                for c in range(LEAD, LEAD + BODY):
                    slot(i, c)

            def turned_hi(i, c):
                act.wait_ge(f_turned, 2 * i + c + 1)
                act.activation(x2T_hi[:, c % 2], job_bank[(c + 1) % 2][:, :], ACT.Copy).then_inc(f_hi, 1)

            def gelu(i, c, f):
                act.wait_ge(f_up, 4 * (2 * i + c) + f + 1)
                if c >= 2:
                    act.wait_ge(f_down, 2 * i + c - 1)
                act.activation(hid[:, c % 2, f], score_bank[f % 2][:, :], ACT.Gelu,
                               bias=bfc[:, f:f + 1]).then_inc(f_gelu, 1)

            def group(i, c):
                for f in range(CHUNKS):
                    if exists(i, c, GROUPS, 2):
                        gelu(i, c, f)
                    if f == 1 and exists(i, c + 1, GROUPS, 2):
                        turned_hi(i, c + 1)

            for c in range(LEAD, LEAD + BODY):
                slot(STEPS // BODY - 1, c)
                if c == 6:
                    act.wait_ge(wm_turned, 1)
                    act.activation(W1_hi[:, :], J0[:, :], ACT.Copy).then_inc(w1_hi_ready, 1)
                if c == 7:
                    turned_hi(0, 0)
            act.wait_ge(ld_lora, 80)
            for c in range(3):
                group(0, c)
            with act.Fori(0, GROUPS // 2 - 2) as i:
                group(i, 3)
                group(i, 4)
            group(GROUPS // 2 - 2, 3)

        @block.vector
        def _(dve):
            def pair_stats(i, c):
                k = 5 * (2 * i + c)
                for r in range(2):
                    dve.bn_stats(stats[:, 2 * (c % 2) + r, :],
                                 X[:, bass.ds((4 * i + 2 * c + r) * P, P)]).then_inc(ln_stats, 1)
                dve.wait_ge(ln_stats, k + 2)
                dve.sem_inc(passed, 1)
                for r in range(2):
                    s = 2 * (c % 2) + r
                    dve.bn_aggr(meanvar[:, s, :], stats[:, s, :]).then_inc(ln_stats, 1)
                dve.wait_ge(ln_stats, k + 4)
                mv = meanvar[:, 2 * (c % 2):2 * (c % 2) + 2, 1]
                dve.tensor_scalar(mv, mv, EPS, None, ALU.add).then_inc(ln_stats, 1)

            def pair_norm(i, c):
                dve.wait_ge(ln_rstd, 2 * i + c + 1)
                for r in range(2):
                    s = 2 * (c % 2) + r
                    n = dve.tensor_scalar(xn[:, c % 2, P * r:P * r + P],
                                          X[:, bass.ds((4 * i + 2 * c + r) * P, P)],
                                          meanvar[:, s, 0:1], rstd[:, s:s + 1],
                                          ALU.subtract, ALU.mult)
                n.then_inc(ln_done, 1)

            def job_lo(i, c, n):
                kind, which = JOB[n]
                if kind == "v":
                    return
                dve.wait_ge(job_hi_done, JOBS * (2 * i + c) + n + 1)
                par, bank = c % 2, bank_of(2 * i + c if isinstance(i, int) else None, n)
                if kind == "turn":
                    cut = slice(2 * P * which, 2 * P * which + 2 * P)
                    dst, hi, src = tT_lo[:, par, cut], tT_hi[:, par, cut], bank[:, 0:2 * P]
                else:
                    cut = slice(2 * which, 2 * which + 2)
                    dst, hi = u_lo[:, par, cut, :], u_hi[:, par, cut, :]
                    src = bank[:, :].rearrange("p (h t) -> p h t", h=2)
                dve.tensor_tensor(dst, src, hi.bitcast(F32), ALU.subtract).then_inc(job_lo_done, 1)

            def batch_bias(i, c):
                dve.scalar_tensor_tensor(out=bias[:, c // 2 % 2, :],
                                         in0=maskb[:, bass.ds((4 * i + c // 2) * P, P)], scalar=-FMAX,
                                         in1=causal[:, :], op0=ALU.mult, op1=ALU.min)\
                    .then_inc(bias_done, 1)

            def mask_max(i, c, g):
                if g == 0:
                    dve.wait_ge(bias_done, 4 * i + c // 2 + 1)
                dve.wait_ge(scores_done, 16 * i + 2 * c + g + 1)
                if c >= 2:
                    dve.wait_ge(exp_done, 16 * i + 2 * (c - 2) + g + 1)
                dve.sem_inc(passed, 1)
                for n in range(4):
                    h = 4 * g + n
                    m = dve.tensor_tensor_reduce(masked[:, c % 2, h, :],
                                                 score_bank[g][:, n * P:n * P + P],
                                                 bias[:, c // 2 % 2, :], 1.0, -FMAX, ALU.add, ALU.max,
                                                 rowmax[:, c % 2, h:h + 1])
                m.then_inc(masked_done, 1)

            def negate_max(i, c):
                dve.wait_ge(masked_done, 16 * i + 2 * c + 2)
                dve.tensor_scalar(negmax[:, c % 2, :], rowmax[:, c % 2, :], -SCALE, None, ALU.mult)\
                    .then_inc(negmax_done, 1)

            def inverse(i, c, g):
                dve.wait_ge(exp_done, 16 * i + 2 * c + g + 1)
                cut = slice(4 * g, 4 * g + 4)
                dve.reciprocal(invsum[:, c % 2, cut], rowsum[:, c % 2, cut]).then_inc(inv_done, 1)

            def probT_copy(i, c):
                dve.wait_ge(turned_done, 16 * i + 2 * c + 2)
                if c >= 2:
                    dve.wait_ge(heads_done, 8 * i + c - 1)
                dve.tensor_copy(probT[:, c % 2, 4:8, :], T1[:, :].rearrange("p (h j) -> p h j", h=4))\
                    .then_inc(probT1_done, 1)

            def headT_copy(i, c):
                dve.wait_ge(heads_done, 8 * i + c + 1)
                dve.tensor_copy(headT[:, c % 2, :], OB[:, :]).then_inc(headT_done, 1)

            def add_y(i, c):
                dve.wait_ge(y_done, 8 * i + c + 1)
                dve.wait_ge(resid_done, 2 * i + c // 4 + 1)
                xb = X[:, bass.ds((4 * i + c // 2) * P, P)]
                dve.tensor_tensor(xb, YB[:, 0:P], xb, ALU.add).then_inc(x_done, 1)

            EARLY_FILL = (4, 5, 6)

            def slot(i, c, filler=None):
                jobs = slot_jobs(i, c)
                if exists(i, c) and c % 2 == 0:
                    batch_bias(i, c)
                before = slot_jobs(i, c - 1)[2:] if c >= 1 else []
                if c % 4 != 3:
                    for pair, n in before:
                        job_lo(i, pair, n)
                if exists(i, c - 2):
                    headT_copy(i, c - 2)
                if exists(i, c - 1) and jobs:
                    inverse(i, c - 1, 1)
                if c % 4 == 3:
                    for pair, n in before:
                        job_lo(i, pair, n)
                if exists(i, c):
                    mask_max(i, c, 0)
                if exists(i, c - 1) and not jobs:
                    inverse(i, c - 1, 1)
                if exists(i, c):
                    mask_max(i, c, 1)
                    negate_max(i, c)
                for pair, n in jobs[0:1]:
                    job_lo(i, pair, n)
                if c % 4 == 3:
                    for pair, n in jobs[1:2]:
                        job_lo(i, pair, n)
                if filler and c in EARLY_FILL:
                    filler()
                if exists(i, c - 1):
                    probT_copy(i, c - 1)
                if c % 4 != 3:
                    for pair, n in jobs[1:2]:
                        job_lo(i, pair, n)
                if exists(i, c):
                    inverse(i, c, 0)
                if filler and c not in EARLY_FILL:
                    filler()
                if c % 2 == 1 and exists(i, c - 2):
                    add_y(i, c - 2)
                if c % 4 == 2 and exists(i, c // 4 + 1, PAIRS, 2):
                    pair_norm(i, c // 4 + 1)
                if c % 4 == 1 and exists(i, c // 4 + 1, PAIRS, 2):
                    pair_stats(i, c // 4 + 1)

            dve.wait_ge(ld_x0, 16)
            pair_stats(0, 0)
            for n in range(2):
                dve.wait_ge(w_turned, n + 3)
                dve.tensor_copy(WkT[:, 4 * n:4 * n + 4, :],
                                turn_bank[n][:, :].rearrange("p (c d) -> p c d", d=P))\
                    .then_inc(wkT_ready, 1)
            pair_norm(0, 0)
            job_lo(0, 0, 0)
            dve.wait_ge(ld_ffn, 32)
            for n in range(2):
                dve.tensor_reduce(wabs[:, n:n + 1], Wf[:, n, :], AX.X, ALU.max,
                                  apply_absolute_value=True).then_inc(wprep, 1)
            for n, bank in enumerate(M_BANKS):
                dve.wait_ge(m_hi_ready, n + 1)
                cut = slice(n % 2 + STEP_HEADS * (n // 2), n % 2 + STEP_HEADS * (n // 2) + 7, 2)
                dve.tensor_tensor(M_lo[:, cut, :], bank[:, :].rearrange("p (h d) -> p h d", d=P),
                                  M_hi[:, cut, :].bitcast(F32), ALU.subtract).then_inc(m_lo_ready, 1)
            for n in range(1, JOBS):
                job_lo(0, 0, n)
                if n == 2:
                    dve.wait_ge(gates_ready, 1)
                    dve.wait_ge(ld_bias, 32)
                    for g in range(2):
                        dve.tensor_scalar(gbias[:, g, :], gbias[:, g, :], gates[:, g:g + 1], None,
                                          ALU.mult).then_inc(gbias_ready, 1)
            job_lo(0, 1, 0)
            dve.wait_ge(wmax_ready, 1)
            dve.tensor_scalar(wscale[:, 0:2], wall[:, :], 1.0 / QMAX, None, ALU.mult).then_inc(wprep, 1)
            dve.wait_ge(wprep, 3)
            dve.reciprocal(wscale[:, 2:4], wscale[:, 0:2]).then_inc(wprep, 1)

            def quantise(n):
                dve.wait_ge(wprep, 4 + 3 * n)
                dve.tensor_scalar(Wt[:, n, :], Wf[:, n, :], wscale[:, 2 + n:3 + n], ROUND,
                                  ALU.mult, ALU.add).then_inc(wprep, 1)
                dve.wait_ge(wprep, 5 + 3 * n)
                dve.tensor_scalar(Wt[:, n, :], Wt[:, n, :], ROUND, QMAX, ALU.subtract, ALU.min)\
                    .then_inc(wprep, 1)
                dve.wait_ge(wprep, 6 + 3 * n)
                dve.tensor_scalar(Wt[:, n, :], Wt[:, n, :], -QMAX - 1, wscale[:, n:n + 1],
                                  ALU.max, ALU.mult).then_inc(wprep, 1)

            dve.wait_ge(ld_mask, 16)
            dve.wait_ge(consts_set, 3)
            for c in range(LEAD):
                slot(0, c)
                if c == 0:
                    dve.wait_ge(ld_wo, 16)
                    dve.tensor_scalar(Wo_sb[:, :, :], Wo_sb[:, :, :], gates[:, 0:1], None, ALU.mult)\
                        .then_inc(wo_ready, 1)
                    quantise(0)
            dve.wait_ge(ld_x1, 16)
            with dve.Fori(0, STEPS // BODY - 1) as i:
                for c in range(LEAD, LEAD + BODY):
                    slot(i, c)

            def lora_b():
                dve.wait_ge(bT_turned, 1)
                dve.tensor_copy(BT[:, 0:FF], J0[0:RANK, :]).then_inc(bT_ready, 1)
                dve.tensor_copy(BT[:, FF:FF + P], J1[0:RANK, 0:P]).then_inc(bT_ready, 1)

            def add_lora():
                dve.wait_ge(wprep, 10)
                dve.wait_ge(lora_ready, 1)
                for n in range(2):
                    dve.scalar_tensor_tensor(out=Wt[:, n, :], in0=job_bank[n][:, :],
                                             scalar=LORA_SCALE, in1=Wt[:, n, :], op0=ALU.mult,
                                             op1=ALU.add).then_inc(wprep, 1)

            def weight_2():
                dve.wait_ge(wm_turned, 1)
                dve.tensor_scalar(W2T[:, :, :], J1[:, :].rearrange("p (c d) -> p c d", d=P),
                                  gates[:, 1:2], None, ALU.mult).then_inc(w12_ready, 1)

            def weight_1():
                dve.wait_ge(w1_hi_ready, 1)
                dve.tensor_tensor(W1_lo[:, :], J0[:, :], W1_hi[:, :].bitcast(F32), ALU.subtract)\
                    .then_inc(w12_ready, 1)

            def group_stats(i, c):
                k = 5 * (2 * i + c)
                for b in range(4):
                    s = dve.bn_stats(stats[:, b, :], X[:, bass.ds((8 * i + 4 * c + b) * P, P)])
                    s.then_inc(f_stats, 1) if b in (1, 3) else None
                dve.wait_ge(f_stats, k + 2)
                dve.sem_inc(passed, 1)
                for b in range(4):
                    s = dve.bn_aggr(meanvar[:, b, :], stats[:, b, :])
                    s.then_inc(f_stats, 1) if b in (1, 3) else None
                dve.wait_ge(f_stats, k + 4)
                dve.tensor_scalar(meanvar[:, :, 1], meanvar[:, :, 1], EPS, None, ALU.add)\
                    .then_inc(f_stats, 1)

            def group_norm(i, c):
                dve.wait_ge(f_rstd, 2 * i + c + 1)
                if c >= 2:
                    dve.wait_ge(f_turned, 2 * i + c - 1)
                for b in range(4):
                    n = dve.tensor_scalar(xn2[c % 2][:, b * P:b * P + P],
                                          X[:, bass.ds((8 * i + 4 * c + b) * P, P)],
                                          meanvar[:, b, 0:1], rstd[:, b:b + 1],
                                          ALU.subtract, ALU.mult)
                n.then_inc(f_norm, 1)

            def turned_lo(i, c):
                dve.wait_ge(f_hi, 2 * i + c + 1)
                dve.tensor_tensor(x2T_lo[:, c % 2], job_bank[(c + 1) % 2][:, :], x2T_hi[:, c % 2].bitcast(F32),
                                  ALU.subtract).then_inc(f_lo, 1)

            def group_out(i, c):
                dve.wait_ge(f_down, 2 * i + c + 1)
                dve.wait_ge(f_resid, 2 * i + c + 1)
                xg = X[:, bass.ds((8 * i + 4 * c) * P, 4 * P)]
                dve.tensor_tensor(xg, turn_bank[c % 2][:, :], xg, ALU.add).then_inc(f_out, 1)

            def group(i, c):
                if exists(i, c + 1, GROUPS, 2):
                    if not (isinstance(i, int) and 2 * i + c == 0):
                        group_stats(i, c + 1)
                        group_norm(i, c + 1)
                    turned_lo(i, c + 1)
                if exists(i, c - 2, GROUPS, 2):
                    group_out(i, c - 2)

            def next_stats():
                dve.wait_ge(x_done, 8)
                group_stats(0, 1)

            fillers = {3: lambda: quantise(1), 4: lora_b, 5: add_lora, 6: weight_2, 7: next_stats}
            for c in range(LEAD, LEAD + BODY):
                slot(STEPS // BODY - 1, c, fillers.get(c))
                if c == 4:
                    dve.wait_ge(x_done, 4)
                    group_stats(0, 0)
                if c == 6:
                    weight_1()
                    group_norm(0, 0)
                if c == 7:
                    turned_lo(0, 0)
                if c == 8:
                    group_norm(0, 1)
            dve.wait_ge(x_done, BATCHES)
            for c in range(3):
                group(0, c)
            with dve.Fori(0, GROUPS // 2 - 2) as i:
                group(i, 3)
                group(i, 4)
            group(GROUPS // 2 - 2, 3)
            group(GROUPS // 2 - 2, 4)
            group(GROUPS // 2 - 2, 5)

        @block.tensor
        def _(pe):
            def split3(dst, w_hi, w_lo, m_hi, m_lo):
                pe.matmul(dst, w_hi, m_hi, start=True, stop=False)
                pe.matmul(dst, w_hi, m_lo, start=False, stop=False)
                return pe.matmul(dst, w_lo, m_hi, start=False, stop=True)

            pe.wait_ge(ident_set, 2)
            for w, loaded, banks in ((Wq_sb, ld_wq, score_bank), (Wk_sb, ld_wk, turn_bank)):
                pe.wait_ge(loaded, 16)
                for n in range(2):
                    for c in range(4):
                        t = pe.transpose(banks[n][:, c * P:c * P + P],
                                         w[:, (4 * n + c) * P:(4 * n + c + 1) * P], ident[:, :])
                    t.then_inc(w_turned, 1)

            def job(i, c, n):
                kind, which = JOB[n]
                par, bank = c % 2, bank_of(2 * i + c if isinstance(i, int) else None, n)
                pair = 2 * i + c
                first = isinstance(i, int) and pair == 0
                if n == 1 and first:
                    pe.wait_ge(m_lo_ready, 2)
                if n == 3 and first:
                    pe.wait_ge(m_lo_ready, 4)
                    pe.wait_ge(wv_lo_ready, 1)
                if first and n >= 6:
                    pe.wait_ge(job_hi_done, n - 5)
                    pe.wait_ge(job_lo_done, splits_before(n - 5))
                if not first:
                    last = JOBS * pair + n - 2
                    pe.wait_ge(job_hi_done, last + 1)
                    if JOB[n - 2][0] != "v":
                        pe.wait_ge(job_lo_done, NSPLIT * pair + (
                            splits_before(n - 1) if n >= 2 else splits_before(JOBS + n - 1) - NSPLIT))
                if kind == "turn":
                    if which == 0:
                        pe.wait_ge(ln_done, pair + 1)
                    else:
                        pe.wait_ge((ld_c0, ld_c1)[par], 16 * (i + c // 2 + 1))
                    for r in range(2):
                        m = pe.transpose(bank[:, r * P:r * P + P],
                                         (xn, C)[which][:, par, r * P:r * P + P], ident[:, :])
                elif kind == "u":
                    pe.wait_ge(job_lo_done, NSPLIT * pair + splits_before(1))
                    for r in range(2):
                        h = 2 * which + r
                        m = split3(bank[:, 256 * r:256 * r + 256], M_hi[:, h, :], M_lo[:, h, :],
                                   tT_hi[:, par, 2 * P:4 * P], tT_lo[:, par, 2 * P:4 * P])
                else:
                    cols = slice(512 * (which % 2), 512 * (which % 2) + 512)
                    keys = slice((2 + which // 2) * P, (3 + which // 2) * P)
                    m = split3(bank[:, :], tT_hi[:, par, keys], tT_lo[:, par, keys],
                               Wv_hi[:, cols], Wv_lo[:, cols])
                m.then_inc(job_done, 1)

            def scores(i, c):
                r, half = c // 2 % 2, c % 2
                par = c // 4 % 2
                pair = 2 * i + c // 4
                pe.wait_ge(job_lo_done, NSPLIT * pair + splits_before(
                    max(JOB.index(("u", 4 * half + 3)), JOB.index(("turn", 0))) + 1))
                if isinstance(i, int) and 8 * i + c == 0:
                    pe.wait_ge(job_hi_done, JOBS - 2)
                    pe.wait_ge(job_lo_done, splits_before(JOBS - 2))
                for g in range(2):
                    if c >= 1:
                        pe.wait_ge(masked_done, 16 * i + 2 * (c - 1) + g + 1)
                    hs = slice(8 * half + 4 * g, 8 * half + 4 * g + 4)
                    split3(score_bank[g][:, :].rearrange("p (h j) -> p h j", h=4),
                           tT_hi[:, par, r * P:r * P + P], tT_lo[:, par, r * P:r * P + P],
                           u_hi[:, par, hs, r * P:r * P + P], u_lo[:, par, hs, r * P:r * P + P])\
                        .then_inc(scores_done, 1)

            def turn(i, c, g):
                pe.wait_ge(prob_done, 16 * i + 2 * c + g + 1)
                if c >= 1:
                    pe.wait_ge((probT0_done, probT1_done)[g], 8 * i + c)
                for n in range(4):
                    t = pe.transpose(turn_bank[g][:, n * P:n * P + P],
                                     prob[:, c % 2, 4 * g + n, :], ident[:, :])
                t.then_inc(turned_done, 1)

            def attend(i, c):
                par, r, half = c // 4 % 2, c // 2 % 2, c % 2
                pe.wait_ge(job_hi_done, JOBS * (2 * i + c // 4) + JOB.index(("v", 2 * r + 1)) + 1)
                if c >= 1:
                    pe.wait_ge(headT_done, 8 * i + c)
                pe.wait_ge(probT0_done, 8 * i + c + 1)
                for h in range(STEP_HEADS):
                    if h == 4:
                        pe.wait_ge(probT1_done, 8 * i + c + 1)
                    rows = slice(DH * (h % 2), DH * (h % 2) + DH)
                    col = (8 * half + h) * DH
                    m = pe.matmul(OB[rows, h // 2 * P:h // 2 * P + P], v[:, par, r, col:col + DH],
                                  probT[:, c % 2, h, :], start=True, stop=True)
                m.then_inc(heads_done, 1)

            def project(i, c):
                half = c % 2
                if half == 0 and c >= 2:
                    pe.wait_ge(x_done, 4 * i + c // 2)
                pe.wait_ge(headT_done, 8 * i + c + 1)
                if isinstance(i, int) and 8 * i + c == 0:
                    pe.wait_ge(wo_ready, 1)
                for q in range(4):
                    m = pe.matmul(YB[:, 0:P], headT[:, c % 2, q * P:q * P + P],
                                  Wo_sb[:, 4 * half + q, :], start=(half == 0 and q == 0),
                                  stop=(half == 1 and q == 3))
                m.then_inc(y_done, 1)

            def slot(i, c, filler=None):
                jobs = slot_jobs(i, c)
                last = jobs[3:] if c % 4 == 2 else []
                if exists(i, c):
                    scores(i, c)
                for pair, n in jobs[0:2]:
                    job(i, pair, n)
                if exists(i, c - 1):
                    turn(i, c - 1, 0)
                if exists(i, c - 1) and jobs:
                    turn(i, c - 1, 1)
                if filler:
                    filler()
                if exists(i, c - 2):
                    project(i, c - 2)
                if exists(i, c - 1) and not jobs:
                    turn(i, c - 1, 1)
                for pair, n in jobs[2:]:
                    if (pair, n) not in last:
                        job(i, pair, n)
                if exists(i, c - 1):
                    attend(i, c - 1)
                for pair, n in last:
                    job(i, pair, n)

            job(0, 0, 0)
            pe.wait_ge(wqT_ready, 2)
            pe.wait_ge(wkT_ready, 2)
            for n, bank in enumerate(M_BANKS):
                rows = slice(DH * (n % 2), DH * (n % 2) + DH)
                for k in range(4):
                    ch = 4 * (n // 2) + k
                    m = pe.matmul(bank[:, k * P:k * P + P], WkT[rows, ch, :], WqT[rows, ch, :],
                                  start=True, stop=True)
                m.then_inc(m_ready, 1)
            for n in range(1, JOBS):
                job(0, 0, n)
            job(0, 1, 0)
            for c in range(LEAD):
                slot(0, c)
            with pe.Fori(0, STEPS // BODY - 1) as i:
                for c in range(LEAD, LEAD + BODY):
                    slot(i, c)

            def lora_b():
                pe.wait_ge(ld_lora, 80)
                pe.wait_ge(job_hi_done, JOBS * PAIRS)
                pe.wait_ge(job_lo_done, NSPLIT * PAIRS)
                for c in range(CHUNKS):
                    pe.transpose(J0[0:RANK, c * P:c * P + P], Bfc[:, c, :], ident[:, :])
                pe.transpose(J1[0:RANK, 0:P], Bpr[:, :], ident[:, :]).then_inc(bT_turned, 1)

            def lora_ba():
                pe.wait_ge(bT_ready, 2)
                for c in range(CHUNKS):
                    pe.matmul(J0[:, c * P:c * P + P], BT[:, c * P:c * P + P], Afc[:, :],
                              start=True, stop=True)
                pe.matmul(J1[:, :], BT[:, FF:FF + P], Apr[:, :], start=True, stop=True)\
                    .then_inc(lora_ready, 1)

            def turn_weights():
                pe.wait_ge(wprep, 12)
                for n in range(2):
                    for c in range(CHUNKS):
                        t = pe.transpose(job_bank[n][:, c * P:c * P + P], Wt[:, n, c * P:c * P + P],
                                         ident[:, :])
                t.then_inc(wm_turned, 1)

            def turn_x(i, c):
                pe.wait_ge(f_norm, 2 * i + c + 1)
                if c < 2:
                    pe.wait_ge(w12_ready, c + 1)
                else:
                    pe.wait_ge(f_lo, 2 * i + c - 1)
                for b in range(4):
                    t = pe.transpose(job_bank[(c + 1) % 2][:, b * P:b * P + P], xn2[c % 2][:, b * P:b * P + P],
                                     ident[:, :])
                t.then_inc(f_turned, 1)

            def up(i, c, f):
                pe.wait_ge(f_lo, 2 * i + c + 1)
                if c >= 1 or f >= 2:
                    pe.wait_ge(f_gelu, 4 * (2 * i + c) + f - 1)
                split3(score_bank[f % 2][:, :], W1_hi[:, f * P:f * P + P], W1_lo[:, f * P:f * P + P],
                       x2T_hi[:, c % 2], x2T_lo[:, c % 2]).then_inc(f_up, 1)

            def down(i, c, t):
                pe.wait_ge(f_gelu, 4 * (2 * i + c) + 4)
                if c >= 2:
                    pe.wait_ge(f_out, 2 * i + c - 1)
                for f in range(CHUNKS):
                    m = pe.matmul(turn_bank[c % 2][:, t * P:t * P + P],
                                  hid[:, c % 2, f, t * P:t * P + P], W2T[:, f, :],
                                  start=(f == 0), stop=(f == CHUNKS - 1))
                if t == 3:
                    m.then_inc(f_down, 1)

            def group(i, c):
                for f in range(CHUNKS):
                    if exists(i, c, GROUPS, 2) and not (c == 0 and f < 2):
                        up(i, c, f)
                    if exists(i, c - 1, GROUPS, 2):
                        down(i, c - 1, f)
                    if f == 1 and c > 0 and exists(i, c + 1, GROUPS, 2):
                        turn_x(i, c + 1)

            def first_ups():
                up(0, 0, 0)
                up(0, 0, 1)

            fillers = {4: lora_b, 5: lora_ba, 6: turn_weights, 7: lambda: turn_x(0, 0),
                       8: first_ups, 9: lambda: turn_x(0, 1)}
            for c in range(LEAD, LEAD + BODY):
                slot(STEPS // BODY - 1, c, fillers.get(c))
            for c in range(3):
                group(0, c)
            with pe.Fori(0, GROUPS // 2 - 2) as i:
                group(i, 3)
                group(i, 4)
            group(GROUPS // 2 - 2, 3)
            group(GROUPS // 2 - 2, 4)


_INS = ["x", "ctx_1024", "mask_BxS2_bf0", "g_xattn", "g_ffn", "L0_xattn_Wq", "L0_xattn_Wk",
        "L0_xattn_Wv", "L0_xattn_Wo", "L0_xattn_bo", "L0_ffn_W_fc", "L0_ffn_b_fc", "L0_ffn_A_fc",
        "L0_ffn_B_fc", "L0_ffn_W_proj", "L0_ffn_b_proj", "L0_ffn_A_proj", "L0_ffn_B_proj"]


def kernel(**inputs):
    import concourse.bacc as bacc
    from concourse.bass_utils import run_bass_kernel_spmd

    nc = bacc.Bacc("TRN2", target_bir_lowering=False, num_devices=1)
    arrays, args = {}, []
    for name in _INS:
        a = np.ascontiguousarray(inputs[name])
        arrays[f"in_{name}"] = a
        args.append(nc.dram_tensor(f"in_{name}", a.shape, mybir.dt.from_np(a.dtype),
                                   kind="ExternalInput").ap())
    args.append(nc.dram_tensor("out", (BATCHES, P, P), F32, kind="ExternalOutput").ap())
    build(nc, *args)
    r = run_bass_kernel_spmd(nc, [arrays], core_ids=[0])
    return r.results[0]["out"]
```
